# Optimizing a Trainium2 kernel written in Bass

```python
import numpy as np
import jax
import jax.numpy as jnp

def _softmax(x, axis=-1):
    return jax.nn.softmax(x, axis=axis)

def _gelu(x):
    return jax.nn.gelu(x, approximate=True)

def _silu(x):
    return jax.nn.silu(x)

def _sigmoid(x):
    return jax.nn.sigmoid(x)

def _layernorm(x, axis=-1, eps=1e-05):
    m = jnp.mean(x, axis=axis, keepdims=True)
    v = jnp.var(x, axis=axis, keepdims=True)
    return (x - m) / jnp.sqrt(v + eps)

def _scatter_add(tgt, idx, src, axis=0):
    return tgt.at[idx].add(src)

def _segment_sum(src, seg, n):
    return jax.ops.segment_sum(src, seg, n)
kernel_name = 'mk_adj_resnorm_d2_adj_r2_41788c'

def setup_inputs(seed: int=0):
    np.random.seed(seed)
    _w = jnp.asarray

    def _rec_inputs():
        import jax
        import jax.numpy as jnp
        _gk = jax.random.key(seed)
        x = -0.0002928 + 1 * jax.random.normal(jax.random.fold_in(_gk, 1), (2048, 256), jnp.float32)
        _a = jax.random.bernoulli(jax.random.fold_in(_gk, 2), 0.00195312, (2048, 2048))
        _a = jnp.logical_or(_a, jnp.swapaxes(_a, -1, -2))
        _a = jnp.logical_or(_a, jnp.eye(2048, dtype=bool))
        _af = _a.astype(jnp.float32)
        _af = _af * jax.random.uniform(jax.random.fold_in(_gk, 3), (2048, 2048), jnp.float32, 0.05, 5.41998)
        adj = _af
        return (x, adj)
    x, adj = _rec_inputs()

    def _L0_gnn_setup():
        import jax, jax.numpy as jnp
        import numpy as np
        N = 4096
        D = 256
        EPS = 1e-12
        key = jax.random.key(seed)
        k1, k2 = jax.random.split(key)
        cur = jax.random.normal(k1, (N, D), dtype=jnp.float32)
        incidence_m = jax.random.normal(k2, (N, N), dtype=jnp.float32)
        return {'cur': cur, 'incidence_m': incidence_m}
    _L0_gnn_all = _L0_gnn_setup()
    _L0_gnn_in = {k: v for k, v in _L0_gnn_all.items() if k in ()}
    del _L0_gnn_all

    def _L1_gnn_setup():
        import jax, jax.numpy as jnp
        import numpy as np
        N = 4096
        D = 256
        key = jax.random.key(seed)
        ks = jax.random.split(key, 6)
        s = 1.0 / np.sqrt(D)
        return {'x': jax.random.normal(ks[0], (N, D), jnp.float32), 'spatial_encoding': jax.random.normal(ks[1], (N, N), jnp.float32), 'edge_encoding': jax.random.normal(ks[2], (N, N), jnp.float32), 'Wq': jax.random.normal(ks[3], (D, D), jnp.float32) * s, 'bq': jnp.zeros((D,), jnp.float32), 'Wk': jax.random.normal(ks[4], (D, D), jnp.float32) * s, 'bk': jnp.zeros((D,), jnp.float32), 'Wv': jax.random.normal(ks[5], (D, D), jnp.float32) * s, 'bv': jnp.zeros((D,), jnp.float32)}
    _L1_gnn_all = _L1_gnn_setup()
    _L1_gnn_in = {k: v for k, v in _L1_gnn_all.items() if k in ('Wq', 'bq', 'Wk', 'bk', 'Wv', 'bv')}
    del _L1_gnn_all
    return {'x': x, 'adj': adj, 'L1_gnn_Wq': _L1_gnn_in['Wq'], 'L1_gnn_bq': _L1_gnn_in['bq'], 'L1_gnn_Wk': _L1_gnn_in['Wk'], 'L1_gnn_bk': _L1_gnn_in['bk'], 'L1_gnn_Wv': _L1_gnn_in['Wv'], 'L1_gnn_bv': _L1_gnn_in['bv']}

def reference(x, adj, L1_gnn_Wq, L1_gnn_bq, L1_gnn_Wk, L1_gnn_bk, L1_gnn_Wv, L1_gnn_bv):
    import jax
    import jax.numpy as jnp

    def _L0_gnn_ref(cur, incidence_m):
        import jax, jax.numpy as jnp
        import numpy as np
        N = 4096
        D = 256
        EPS = 1e-12
        mask = incidence_m > 0
        head = jax.lax.stop_gradient(mask.astype(incidence_m.dtype))
        head = head / jnp.maximum(jnp.sqrt(jnp.sum(head * head, axis=-1, keepdims=True)), EPS)
        inc = incidence_m + head
        edge_fea = inc @ cur
        edge_degree = jnp.sum(inc, axis=-1, keepdims=True)
        return edge_fea / edge_degree

    def _L1_gnn_ref(x, spatial_encoding, edge_encoding, Wq, bq, Wk, bk, Wv, bv):
        import jax, jax.numpy as jnp
        import numpy as np
        N = 4096
        D = 256
        q = x @ Wq.T + bq
        k = x @ Wk.T + bk
        v = x @ Wv.T + bv
        scale = 1.0 / jnp.sqrt(jnp.asarray(q.shape[-1], q.dtype))
        a = q @ k.T * scale + spatial_encoding + edge_encoding
        attn = jax.nn.softmax(a, axis=-1)
        return attn @ v
    x = _layernorm(x + _L0_gnn_ref(x, adj), axis=-1)
    x = _layernorm(x + _L1_gnn_ref(x, adj, adj, L1_gnn_Wq, L1_gnn_bq, L1_gnn_Wk, L1_gnn_bk, L1_gnn_Wv, L1_gnn_bv), axis=-1)
    return x

_drawn_inputs = setup_inputs


def setup_inputs(seed=0):
    import zlib

    import numpy as np

    out = dict(_drawn_inputs(seed))
    spreads = {'L1_gnn_bq': (0.0, 0.332), 'L1_gnn_bk': (0.0, 0.8), 'L1_gnn_bv': (0.0, 0.1)}
    factors = {}
    for name, (base, spread) in spreads.items():
        noise = np.random.default_rng([zlib.crc32(name.encode()), seed]).standard_normal(out[name].shape)
        drawn = base * np.exp(spread * noise) if base else spread * noise
        out[name] = jnp.asarray(drawn.astype(out[name].dtype))
    for name, factor in factors.items():
        out[name] = (out[name] * factor).astype(out[name].dtype)
    return out
```

```python
from contextlib import ExitStack

import numpy as np

import concourse.bass as bass
from concourse import mybir

F32 = mybir.dt.float32
F16 = mybir.dt.float16
BF16 = mybir.dt.bfloat16
ALU = mybir.AluOpType
ACT = mybir.ActivationFunctionType
AX = mybir.AxisListType

P = 128
LANES = 4
BANK = LANES * P

X_SCALE = 1.0 / 8
W_SCALE = 16.0
Y_SCALE = 1.0 / 4
P_SHIFT = 12 * float(np.log(2.0))
LN_EPS = 1e-5
HEAD_EPS = 1e-12


def gnn_layers(nc, x, adj, wq, wk, wv_t, bq, bk, bv, out):
    N, D = x.shape
    NT = N // P
    KD = D // P
    NG = NT // LANES
    HALF = N // 2
    DEG_SCALE = 1.0 / (2.0 * float(np.sqrt(D)))
    assert N % BANK == 0 and KD == 2 and NT % 2 == 0 and NG % 2 == 0
    assert X_SCALE * Y_SCALE == DEG_SCALE

    with ExitStack() as ctx:
        def sb(name, shape, dt=F32):
            return ctx.enter_context(nc.sbuf_tensor(name, shape, dt))

        def ps(name, shape, dt=F32):
            return ctx.enter_context(nc.psum_tensor(name, shape, dt))

        def sem(name):
            return ctx.enter_context(nc.semaphore(name))

        ident = sb("ident", [P, P])
        ones = sb("ones", [P, P])
        minus_half = sb("minus_half", [P, 1])
        xs = sb("xs", [P, NT, D])
        x_split = sb("x_split", [P, NT, 2 * D], F16)
        wq_s = sb("wq_s", [P, KD, D])
        wk_s = sb("wk_s", [P, KD, D])
        wv_s = sb("wv_s", [P, KD, D])
        bq_s = sb("bq_s", [P, KD])
        bk_s = sb("bk_s", [P, KD])
        bv_s = sb("bv_s", [P, D])
        bq_wide = sb("bq_wide", [P, KD, P])
        g_hi = sb("g_hi", [P, KD, D], F16)
        g_lo = sb("g_lo", [P, KD, D], F16)
        y_bias = sb("y_bias", [P, KD])
        wv_u = sb("wv_u", [P, KD, D + 2])
        wv_hi = sb("wv_hi", [P, KD, D + 2], F16)
        wv_lo = sb("wv_lo", [P, KD, D + 2], F16)
        c_bias = sb("c_bias", [P, 1])

        adj_s = [sb(f"adj_s{i}", [P, N]) for i in range(2)]
        mask = sb("mask", [P, N], BF16)
        mask_copy = sb("mask_copy", [P, N], BF16)
        inc = [sb(f"inc{i}", [P, N]) for i in range(2)]
        t_hi = [sb(f"t_hi{i}", [P, NT, P], F16) for i in range(2)]
        t_lo = [sb(f"t_lo{i}", [P, NT, P], F16) for i in range(2)]
        count = sb("count", [P, 2])
        head_r = sb("head_r", [P, 2])
        deg_parts = [sb(f"deg_parts{i}", [P, 2]) for i in range(2)]
        deg = sb("deg", [P, 1])
        deg_r = sb("deg_r", [P, 1])
        z_half = sb("z_half", [P, D])
        z = sb("z", [P, D])
        stats = sb("stats", [P, 6])
        mv = sb("mv", [P, 2])
        var_eps = sb("var_eps", [P, 1])
        rstd = sb("rstd", [P, 1])
        x1_t = [sb(f"x1_t{i}", [P, D]) for i in range(2)]
        xt_hi = sb("xt_hi", [P, KD, N], F16)
        xt_lo = sb("xt_lo", [P, KD, N], F16)
        v_f = sb("v_f", [P, D])
        v_split = sb("v_split", [P, NT, 2 * D], F16)
        c_row = sb("c_row", [P, NT])
        y_f = sb("y_f", [P, KD, P])
        yt_hi = [sb(f"yt_hi{i}", [P, KD, P], F16) for i in range(2)]
        yt_lo = [sb(f"yt_lo{i}", [P, KD, P], F16) for i in range(2)]
        score, prob = inc
        chunk_max = sb("chunk_max", [P, NG])
        row_max = sb("row_max", [P, 1])
        top = sb("top", [P, 1])
        exp_bias = sb("exp_bias", [P, 1])
        den = [sb(f"den{i}", [P, 1]) for i in range(2)]
        den_r = sb("den_r", [P, 1])
        out_t = [sb(f"out_t{i}", [P, D]) for i in range(2)]

        ps_t = [ps(f"ps_t{i}", [P, BANK]) for i in range(2)]
        ps_o = [ps(f"ps_o{i}", [P, 2 * D]) for i in range(2)]
        ps_s = [ps(f"ps_s{i}", [P, BANK]) for i in range(2)]
        ps_y = ps("ps_y", [P, BANK])
        ps_w = ps("ps_w", [P, BANK])
        ps_xt, ps_v = ps_s

        adj_loaded = [sem(f"adj_loaded{i}") for i in range(2)]
        adj_used = sem("adj_used")
        x_loaded = sem("x_loaded")
        w_loaded = sem("w_loaded")
        const_ready = sem("const_ready")
        ident_ready = sem("ident_ready")
        x_hi_done = sem("x_hi_done")
        x_split_done = sem("x_split_done")
        bq_wide_done = sem("bq_wide_done")
        g_done = sem("g_done")
        g_hi_done = sem("g_hi_done")
        g_split_done = sem("g_split_done")
        wv_u_done = sem("wv_u_done")
        wv_hi_done = sem("wv_hi_done")
        mask_done = sem("mask_done")
        count_done = sem("count_done")
        head_floor = sem("head_floor")
        head_done = sem("head_done")
        inc_done = sem("inc_done")
        trans_done = sem("trans_done")
        hi_done = sem("hi_done")
        lo_done = sem("lo_done")
        prod_done = sem("prod_done")
        deg_done = sem("deg_done")
        deg_r_done = sem("deg_r_done")
        z_half_done = sem("z_half_done")
        z_done = sem("z_done")
        stats_done = sem("stats_done")
        mv_done = sem("mv_done")
        var_done = sem("var_done")
        rstd_done = sem("rstd_done")
        x1_done = sem("x1_done")
        x1_kept = sem("x1_kept")
        xt_done = sem("xt_done")
        xt_hi_done = sem("xt_hi_done")
        xt_lo_done = sem("xt_lo_done")
        v_done = sem("v_done")
        v_f_done = sem("v_f_done")
        v_hi_done = sem("v_hi_done")
        v_lo_done = sem("v_lo_done")
        y_done = sem("y_done")
        y_f_done = sem("y_f_done")
        y_hi_done = sem("y_hi_done")
        y_lo_done = sem("y_lo_done")
        qk_done = sem("qk_done")
        score_done = sem("score_done")
        row_max_done = sem("row_max_done")
        top_done = sem("top_done")
        bias_done = sem("bias_done")
        exp_done = sem("exp_done")
        den_r_done = sem("den_r_done")
        out_ready = sem("out_ready")
        out_stored = [sem(f"out_stored{i}") for i in range(2)]

        adj_rows = adj.rearrange("(t p) n -> t p n", p=P)
        out_rows = out.rearrange("(t p) d -> t p d", p=P)

        def wait_apart(eng, reg, awaited, value, settled):
            eng.reg_mov(reg, value)
            eng.wait_ge(settled, 1)
            eng.wait_ge(awaited, reg)

        block = ctx.enter_context(nc.Block())

        @block.sync
        def _(sp):
            def load_adj(t, b, n=None):
                if n is not None:
                    sp.wait_ge(adj_used, n - 1)
                sp.dma_start(adj_s[b][:, :], adj_rows[t, :, :]).then_inc(adj_loaded[b], 16)

            def store_out(t, b):
                sp.wait_ge(out_ready, t + 1)
                sp.dma_start(out_rows[t, :, :], out_t[b][:, :]).then_inc(out_stored[b], 16)

            load_adj(0, 0)
            load_adj(1, 1)
            with sp.Fori(2, NT - 1, 2) as t:
                for b in range(2):
                    load_adj(t + b, b, t + b)
            for b in range(2):
                load_adj(b, b, NT + b)
            with sp.Fori(2, NT - 1, 2) as t:
                for b in range(2):
                    load_adj(t + b, b, t + b + NT)
                    store_out(t + b - 2, b)
            for b in range(2):
                store_out(NT - 2 + b, b)
                sp.wait_ge(out_stored[b], 16 * (NT // 2))

        @block.gpsimd
        def _(pool):
            nc.gpsimd.memset(minus_half[:, :], -0.5).then_inc(const_ready, 1)
            nc.gpsimd.memset(ones[:, :], 1.0).then_inc(const_ready, 1)
            nc.gpsimd.memset(ident[:, :], 0.0).then_inc(const_ready, 1)
            pool.wait_ge(const_ready, 3)
            nc.gpsimd.affine_select(out=ident[:, :], in_=ident[:, :], compare_op=ALU.not_equal, fill=1.0,
                                    base=0, pattern=[[-1, P]], channel_multiplier=1).then_inc(ident_ready, 1)

            pool_value = pool.alloc_register("pool_value")

            def head_norm(t, b):
                wait_apart(pool, pool_value, count_done, t + 1, const_ready)
                nc.gpsimd.tensor_scalar(head_r[:, b:b + 1], count[:, b:b + 1], HEAD_EPS ** 2, None,
                                        ALU.max).then_inc(head_floor, 1)
                pool.wait_ge(head_floor, t + 1)
                nc.gpsimd.tensor_tensor(head_r[:, b:b + 1], head_r[:, b:b + 1], minus_half[:, :],
                                        ALU.pow).then_inc(head_done, 1)

            def row_rstd(n):
                pool.wait_ge(var_done, n + 1)
                nc.gpsimd.tensor_tensor(rstd[:, :], var_eps[:, :], minus_half[:, :],
                                        ALU.pow).then_inc(rstd_done, 1)

            def keep_x1(t, b):
                pool.wait_ge(x1_done, t + 1)
                nc.gpsimd.tensor_copy(xs[:, bass.ds(t, 1), :], x1_t[b][:, :]).then_inc(x1_kept, 1)

            head_norm(0, 0)
            head_norm(1, 1)
            head_norm(2, 0)
            with pool.Fori(0, NT - 5, 2) as t:
                for b in range(2):
                    head_norm(t + b + 3, 1 - b)
                    row_rstd(t + b)
                    keep_x1(t + b, b)
            head_norm(NT - 1, 1)
            for t in range(NT - 4, NT):
                row_rstd(t)
                keep_x1(t, t % 2)
            with pool.Fori(0, NT) as t:
                row_rstd(t + NT)

        @block.tensor
        def _(pe):
            def weights():
                pe.wait_ge(w_loaded, 16 * 6)
                pe.wait_ge(bq_wide_done, KD)
                for m in range(KD):
                    for k in range(KD):
                        nc.tensor.matmul(ps_w[:, m * D:(m + 1) * D], wq_s[:, k, m * P:(m + 1) * P],
                                         wk_s[:, k, :], start=(k == 0), stop=(k == KD - 1))
                for m in range(KD):
                    for k in range(KD):
                        nc.tensor.matmul(ps_y[:, m:m + 1], wk_s[:, k, m * P:(m + 1) * P], bq_s[:, k:k + 1],
                                         start=(k == 0), stop=(k == KD - 1))
                for m in range(KD):
                    for k in range(KD):
                        nc.tensor.matmul(ps_y[:, KD + m:KD + m + 1], wq_s[:, k, m * P:(m + 1) * P],
                                         bk_s[:, k:k + 1], start=(k == 0), stop=(k == KD - 1))
                for k in range(KD):
                    last = nc.tensor.matmul(ps_y[:, 2 * KD:2 * KD + 1], bq_wide[:, k, :], bk_s[:, k:k + 1],
                                            start=(k == 0), stop=(k == KD - 1))
                last.then_inc(g_done, 1)

            def transpose_group(src, n, g):
                if n is not None:
                    pe.wait_ge(lo_done, n - 1)
                for i in range(LANES):
                    c = (g * LANES + i) * P
                    last = nc.tensor.transpose(ps_t[g % 2][:, i * P:(i + 1) * P], src[:, c:c + P], ident[:, :])
                last.then_inc(trans_done, 1)

            def product_group(b, g, right):
                for i in range(LANES):
                    j = g * LANES + i
                    for wide in (True, False) if j == 0 else (False, True):
                        left, cols = (t_hi[b], 2 * D) if wide else (t_lo[b], D)
                        last = nc.tensor.matmul(ps_o[b][:, 0:cols], left[:, j, :], right[:, j, 0:cols],
                                                start=(wide and j == 0), stop=(wide and j == NT - 1),
                                                skip_group_check=True)
                if g == NG - 1:
                    last.then_inc(prod_done, 1)

            def x1_transpose(t, b, first=False):
                pe.wait_ge(x1_done, t + 1)
                if not first:
                    pe.wait_ge(xt_lo_done, t)
                for k in range(KD):
                    last = nc.tensor.transpose(ps_xt[:, k * P:(k + 1) * P], x1_t[b][:, k * P:(k + 1) * P],
                                               ident[:, :])
                last.then_inc(xt_done, 1)

            def v_product(t, first=False):
                pe.wait_ge(xt_lo_done, t + 1)
                if not first:
                    pe.wait_ge(v_f_done, t)
                for k in range(KD):
                    hi = xt_hi[:, k, bass.ts(t, P)]
                    lo = xt_lo[:, k, bass.ts(t, P)]
                    for a, (left, right) in enumerate(((hi, wv_hi), (hi, wv_lo), (lo, wv_hi))):
                        last = nc.tensor.matmul(ps_v[:, 0:D + 2], left, right[:, k, :],
                                                start=(k == 0 and a == 0), stop=(k == KD - 1 and a == 2))
                last.then_inc(v_done, 1)

            def layer1_step(t, b, trans=True, prod=True, xt=True, v=True, first=False):
                for g in range(NG):
                    if trans:
                        if g % 2 == 0:
                            pe.wait_ge(inc_done, 2 * t + g // 2 + 1)
                        transpose_group(inc[b], None if first and g < 2 else t * NG + g, g)
                    if prod:
                        pe.wait_ge(lo_done, t * NG + (g + 1 - NG))
                        if g == 0 and xt:
                            pe.wait_ge(z_done, t - 1)
                        product_group(1 - b, g, x_split)
                if xt:
                    x1_transpose(t - 2, b, first=not v)
                if v:
                    v_product(t - 3, first=(v == "first"))

            pe.wait_ge(ident_ready, 1)
            weights()
            layer1_step(0, 0, prod=False, xt=False, v=False, first=True)
            pe.wait_ge(x_split_done, NG)
            layer1_step(1, 1, xt=False, v=False)
            layer1_step(2, 0, v=False)
            pe.wait_ge(wv_hi_done, 2)
            layer1_step(3, 1, v="first")
            with pe.Fori(4, NT - 1, 2) as t:
                for b in range(2):
                    layer1_step(t + b, b)
            layer1_step(NT, 0, trans=False)
            layer1_step(NT + 1, 1, trans=False, prod=False)
            v_product(NT - 1)

            def y_product(t, b, first=False):
                if not first:
                    pe.wait_ge(y_f_done, t * KD)
                for m in range(KD):
                    for k in range(KD):
                        xh = xt_hi[:, k, bass.ts(t, P)]
                        xl = xt_lo[:, k, bass.ts(t, P)]
                        gs = slice(m * P, (m + 1) * P)
                        for a, (left, right) in enumerate(((g_hi, xh), (g_hi, xl), (g_lo, xh))):
                            last = nc.tensor.matmul(ps_y[:, gs], left[:, k, gs], right,
                                                    start=(k == 0 and a == 0), stop=(k == KD - 1 and a == 2))
                last.then_inc(y_done, 1)

            def qk_chunk(t, b, c, first):
                if c == 0:
                    pe.wait_ge(y_lo_done, t + 1)
                if not first:
                    pe.wait_ge(score_done, t * NG + (c - 1))
                cs = slice(c * BANK, (c + 1) * BANK)
                for k in range(KD):
                    for a, (left, right) in enumerate(((yt_hi[b], xt_hi), (yt_hi[b], xt_lo), (yt_lo[b], xt_hi))):
                        last = nc.tensor.matmul(ps_s[c % 2][:, :], left[:, k, :], right[:, k, cs],
                                                start=(k == 0 and a == 0), stop=(k == KD - 1 and a == 2))
                last.then_inc(qk_done, 1)

            def layer2_step(t, b, qk=True, pv=True, y=True):
                for c in range(NG):
                    if qk:
                        qk_chunk(t, b, c, first=(not pv and c < 2))
                    if pv:
                        if c == 0:
                            pe.wait_ge(exp_done, t)
                        transpose_group(prob, (t + (NT - 1)) * NG + c, c)
                if y:
                    y_product(t + 1, 1 - b)
                if pv:
                    pe.wait_ge(z_done, t + (NT - 2))
                    for g in range(NG):
                        pe.wait_ge(lo_done, (t + (NT - 1)) * NG + g + 1)
                        product_group(1 - b, g, v_split)

            pe.wait_ge(g_split_done, KD)
            y_product(0, 0, first=True)
            pe.wait_ge(v_f_done, NT)
            layer2_step(0, 0, pv=False)
            pe.wait_ge(v_lo_done, NT)
            layer2_step(1, 1)
            with pe.Fori(2, NT - 3, 2) as t:
                for b in range(2):
                    layer2_step(t + b, b)
            layer2_step(NT - 2, 0)
            layer2_step(NT - 1, 1, y=False)
            layer2_step(NT, 0, qk=False, y=False)

        @block.scalar
        def _(act):
            for name, src in ((wq_s, wq), (wk_s, wk), (wv_s, wv_t)):
                act.dma_start(name[:, :, :], src.rearrange("(k p) d -> p k d", p=P)).then_inc(w_loaded, 16)
            act.dma_start(bq_s[:, :], bq).then_inc(w_loaded, 16)
            act.dma_start(bk_s[:, :], bk).then_inc(w_loaded, 16)
            act.dma_start(bv_s[:, :], bv).then_inc(w_loaded, 16)
            act.dma_start(xs[:, :, :], x.rearrange("(t p) d -> p t d", p=P)).then_inc(x_loaded, 16)

            def count_heads(t, b):
                act.wait_ge(mask_done, t + 1)
                nc.scalar.activation(mask_copy[:, :], mask[:, :], ACT.Copy,
                                     accum_out=count[:, b:b + 1]).then_inc(count_done, 1)

            def hi_group(n, b, g):
                act.wait_ge(trans_done, n + 1)
                nc.scalar.copy(t_hi[b][:, g * LANES:(g + 1) * LANES, :], ps_t[g % 2][:, :]).then_inc(hi_done, 1)

            def xt_hi_tile(t):
                act.wait_ge(xt_done, t + 1)
                nc.scalar.activation(xt_hi[:, :, bass.ts(t, P)],
                                     ps_xt[:, 0:KD * P].rearrange("p (k n) -> p k n", k=KD),
                                     ACT.Copy, scale=X_SCALE).then_inc(xt_hi_done, 1)

            def v_hi_tile(t):
                act.wait_ge(v_f_done, t + 1)
                nc.scalar.copy(v_split[:, bass.ds(t, 1), 0:D], v_f[:, :]).then_inc(v_hi_done, 1)

            def layer1_step(t, b, trans=True, count=True, xt=True, v=True, reuse=True):
                if xt:
                    xt_hi_tile(t - 3)
                if v:
                    v_hi_tile(t - 4)
                if trans:
                    if reuse:
                        act.wait_ge(prod_done, t - 1)
                    for g in range(NG):
                        hi_group(t * NG + g, b, g)
                        if g == 1 and count:
                            count_heads(t + 1, 1 - b)

            count_heads(0, 0)
            act.wait_ge(g_done, 1)
            for m in range(KD):
                nc.scalar.activation(g_hi[:, m, :], ps_w[:, m * D:(m + 1) * D], ACT.Copy,
                                     scale=W_SCALE).then_inc(g_hi_done, 1)
            act.wait_ge(wv_u_done, 2 * KD)
            nc.scalar.copy(wv_hi[:, :, :], wv_u[:, :, :]).then_inc(wv_hi_done, 1)
            act.wait_ge(x_loaded, 16)
            for g in range(NG):
                ts = slice(g * LANES, (g + 1) * LANES)
                nc.scalar.copy(x_split[:, ts, 0:D], xs[:, ts, :]).then_inc(x_hi_done, 1)
            for t in range(4):
                layer1_step(t, t % 2, xt=(t == 3), v=False, reuse=(t >= 2))
            with act.Fori(4, NT - 3, 2) as t:
                for b in range(2):
                    layer1_step(t + b, b)
            layer1_step(NT - 2, 0)
            layer1_step(NT - 1, 1, count=False)
            for t in range(NT, NT + 4):
                layer1_step(t, t % 2, trans=False, xt=(t < NT + 3))

            def y_tile(t, b):
                act.wait_ge(y_done, t + 1)
                act.wait_ge(y_lo_done, t)
                for m in range(KD):
                    nc.scalar.activation(y_f[:, m, :], ps_y[:, m * P:(m + 1) * P], ACT.Identity,
                                         scale=Y_SCALE / (X_SCALE * W_SCALE),
                                         bias=y_bias[:, m:m + 1]).then_inc(y_f_done, 1)
                act.wait_ge(y_f_done, KD * t + KD)
                nc.scalar.copy(yt_hi[b][:, :, :], y_f[:, :, :]).then_inc(y_hi_done, 1)

            def layer2_step(t, b, qk=True, pv=True, y=True):
                if pv:
                    for g in range(NG):
                        hi_group((t + (NT - 1)) * NG + g, 1 - b, g)
                if qk:
                    act.wait_ge(bias_done, t + 1)
                    if pv:
                        act.wait_ge(trans_done, (t + NT) * NG)
                    nc.scalar.activation(prob[:, :], score[:, :], ACT.Exp, scale=2.0, bias=exp_bias[:, :],
                                         accum_out=den[b][:, :]).then_inc(exp_done, 1)
                if y:
                    y_tile(t + 1, 1 - b)

            act.wait_ge(y_done, 1)
            for m in range(KD):
                nc.scalar.activation(y_f[:, m, :], ps_y[:, m * P:(m + 1) * P], ACT.Identity,
                                     scale=Y_SCALE / (X_SCALE * W_SCALE),
                                     bias=y_bias[:, m:m + 1]).then_inc(y_f_done, 1)
            act.wait_ge(y_f_done, KD)
            nc.scalar.copy(yt_hi[0][:, :, :], y_f[:, :, :]).then_inc(y_hi_done, 1)
            layer2_step(0, 0, pv=False)
            layer2_step(1, 1)
            with act.Fori(2, NT - 3, 2) as t:
                for b in range(2):
                    layer2_step(t + b, b)
            layer2_step(NT - 2, 0)
            layer2_step(NT - 1, 1, y=False)
            layer2_step(NT, 0, qk=False, y=False)

        @block.vector
        def _(dve):
            dve_value = dve.alloc_register("dve_value")

            def mask_tile(t, b, first=False):
                dve.wait_ge(adj_loaded[b], (t + 2 - b) * 8)
                if not first:
                    dve.wait_ge(inc_done, 2 * t)
                    dve.wait_ge(count_done, t)
                nc.vector.tensor_scalar(mask[:, :], adj_s[b][:, :], 0.0, None, ALU.is_gt).then_inc(mask_done, 1)

            def inc_half(t, b, h, reuse=True):
                dve.wait_ge(head_done, t + 1)
                if h == 0 and reuse:
                    dve.wait_ge(trans_done, (t - 1) * NG)
                hs = slice(h * HALF, (h + 1) * HALF)
                ins = nc.vector.scalar_tensor_tensor(
                    out=inc[b][:, hs], in0=mask[:, hs], scalar=head_r[:, b:b + 1], in1=adj_s[b][:, hs],
                    op0=ALU.mult, op1=ALU.add, accum_out=deg_parts[b][:, h:h + 1])
                ins.then_inc(inc_done, 1)
                if h == 1:
                    dve.wait_ge(inc_done, 2 * t + 2)
                    dve.sem_inc(adj_used, 1)

            def lo_group(n, b, g):
                dve.wait_ge(hi_done, n + 1)
                nc.vector.tensor_tensor(t_lo[b][:, g * LANES:(g + 1) * LANES, :],
                                        ps_t[g % 2][:, :].rearrange("p (a n) -> p a n", a=LANES),
                                        t_hi[b][:, g * LANES:(g + 1) * LANES, :],
                                        ALU.subtract).then_inc(lo_done, 1)

            def residual(n, base, b, scale, t):
                dve.wait_ge(prod_done, n + 1)
                nc.vector.scalar_tensor_tensor(out=z_half[:, :], in0=ps_o[b][:, D:2 * D], scalar=scale,
                                               in1=base, op0=ALU.mult, op1=ALU.add).then_inc(z_half_done, 1)
                dve.wait_ge(z_half_done, n + 1)
                nc.vector.scalar_tensor_tensor(out=z[:, :], in0=ps_o[b][:, 0:D], scalar=scale,
                                               in1=z_half[:, :], op0=ALU.mult, op1=ALU.add).then_inc(z_done, 1)
                dve.wait_ge(z_done, n + 1)
                nc.vector.bn_stats(stats[:, :], z[:, :]).then_inc(stats_done, 1)
                wait_apart(dve, dve_value, stats_done, n + 1, const_ready)
                nc.vector.bn_aggr(mv[:, :], stats[:, :]).then_inc(mv_done, 1)
                dve.wait_ge(mv_done, n + 1)
                nc.vector.tensor_scalar(var_eps[:, :], mv[:, 1:2], LN_EPS, None, ALU.add).then_inc(var_done, 1)

            def normalise(n, dst, done):
                dve.wait_ge(rstd_done, n + 1)
                nc.vector.tensor_scalar(dst, z[:, :], mv[:, 0:1], rstd[:, :], ALU.subtract,
                                        ALU.mult).then_inc(done, 1)

            def edge(t, b):
                residual(t, xs[:, bass.ds(t, 1), :], b, deg_r[:, :], t)

            def degree(t, b):
                dve.wait_ge(inc_done, 2 * t + 2)
                nc.vector.tensor_tensor(deg[:, :], deg_parts[b][:, 0:1], deg_parts[b][:, 1:2],
                                        ALU.add).then_inc(deg_done, 1)
                dve.wait_ge(deg_done, t + 1)
                nc.vector.reciprocal(deg_r[:, :], deg[:, :]).then_inc(deg_r_done, 1)
                dve.wait_ge(deg_r_done, t + 1)

            def x1_tile(t, b, reuse=True):
                if reuse:
                    dve.wait_ge(xt_done, t - 1)
                    dve.wait_ge(x1_kept, t - 1)
                normalise(t, x1_t[b][:, :], x1_done)

            def xt_lo_tile(t):
                dve.wait_ge(xt_hi_done, t + 1)
                nc.vector.scalar_tensor_tensor(out=xt_lo[:, :, bass.ts(t, P)],
                                               in0=ps_xt[:, 0:KD * P].rearrange("p (k n) -> p k n", k=KD),
                                               scalar=X_SCALE, in1=xt_hi[:, :, bass.ts(t, P)],
                                               op0=ALU.mult, op1=ALU.subtract).then_inc(xt_lo_done, 1)

            def v_tile(t, first=False):
                dve.wait_ge(v_done, t + 1)
                if not first:
                    dve.wait_ge(v_lo_done, t)
                nc.vector.tensor_scalar(c_row[:, bass.ds(t, 1)], ps_v[:, D:D + 1],
                                        2 * DEG_SCALE / (X_SCALE * W_SCALE), c_bias[:, :], ALU.mult, ALU.add)
                nc.vector.scalar_tensor_tensor(out=v_f[:, :], in0=ps_v[:, 0:D], scalar=1.0 / (X_SCALE * W_SCALE),
                                               in1=bv_s[:, :], op0=ALU.mult, op1=ALU.add).then_inc(v_f_done, 1)

            def v_lo_tile(t):
                dve.wait_ge(v_hi_done, t + 1)
                nc.vector.tensor_tensor(v_split[:, bass.ds(t, 1), D:2 * D], v_f[:, :],
                                        v_split[:, bass.ds(t, 1), 0:D], ALU.subtract).then_inc(v_lo_done, 1)

            def layer1_step(t, b, trans=True, ahead=True, deg=True, z=True, xt=True, v=True, first=False):
                if xt:
                    xt_lo_tile(t - 3)
                if v:
                    v_tile(t - 4, first=(v == "first"))
                if trans:
                    lo_group(t * NG, b, 0)
                if ahead:
                    mask_tile(t + 1, 1 - b)
                if z:
                    edge(t - 2, b)
                if deg:
                    degree(t - 1, 1 - b)
                if trans:
                    lo_group(t * NG + 1, b, 1)
                if v:
                    v_lo_tile(t - 4)
                if trans:
                    lo_group(t * NG + 2, b, 2)
                if ahead:
                    inc_half(t + 1, 1 - b, 0, reuse=not first)
                if z:
                    x1_tile(t - 2, b, reuse=xt and v)
                if trans:
                    lo_group(t * NG + 3, b, 3)
                if ahead:
                    inc_half(t + 1, 1 - b, 1)

            mask_tile(0, 0, first=True)
            dve.wait_ge(w_loaded, 16 * 6)
            dve.wait_ge(const_ready, 2)
            for k in range(KD):
                nc.vector.tensor_scalar(bq_wide[:, k, :], ones[:, :], bq_s[:, k:k + 1], None,
                                        ALU.mult).then_inc(bq_wide_done, 1)
                nc.vector.tensor_scalar(wv_u[:, k, 0:D], wv_s[:, k, :], W_SCALE, None,
                                        ALU.mult).then_inc(wv_u_done, 1)
            inc_half(0, 0, 0, reuse=False)
            inc_half(0, 0, 1)
            dve.wait_ge(g_done, 1)
            nc.vector.tensor_scalar(y_bias[:, :], ps_y[:, 0:KD], Y_SCALE, None, ALU.mult)
            nc.vector.tensor_scalar(c_bias[:, :], ps_y[:, 2 * KD:2 * KD + 1], 2 * DEG_SCALE, None, ALU.mult)
            for k in range(KD):
                nc.vector.tensor_scalar(wv_u[:, k, D:D + 2], ps_y[:, KD + k:KD + k + 1].to_broadcast([P, 2]),
                                        W_SCALE, None, ALU.mult).then_inc(wv_u_done, 1)
            dve.wait_ge(g_hi_done, KD)
            for m in range(KD):
                nc.vector.scalar_tensor_tensor(out=g_lo[:, m, :], in0=ps_w[:, m * D:(m + 1) * D], scalar=W_SCALE,
                                               in1=g_hi[:, m, :], op0=ALU.mult,
                                               op1=ALU.subtract).then_inc(g_split_done, 1)
            dve.wait_ge(wv_hi_done, 1)
            nc.vector.tensor_tensor(wv_lo[:, :, :], wv_u[:, :, :], wv_hi[:, :, :], ALU.subtract).then_inc(wv_hi_done, 1)
            for g in range(NG):
                ts = slice(g * LANES, (g + 1) * LANES)
                dve.wait_ge(x_hi_done, g + 1)
                nc.vector.tensor_tensor(x_split[:, ts, D:2 * D], xs[:, ts, :], x_split[:, ts, 0:D],
                                        ALU.subtract).then_inc(x_split_done, 1)
            for t in range(4):
                layer1_step(t, t % 2, deg=(t >= 1), z=(t >= 2), xt=(t == 3), v=False, first=(t == 0))
            layer1_step(4, 0, v="first")
            layer1_step(5, 1)
            with dve.Fori(6, NT - 3, 2) as t:
                for b in range(2):
                    layer1_step(t + b, b)
            layer1_step(NT - 2, 0)
            layer1_step(NT - 1, 1, ahead=False)
            for t in range(NT, NT + 4):
                layer1_step(t, t % 2, trans=False, ahead=False, deg=(t == NT), z=(t < NT + 2), xt=(t < NT + 3))

            def score_chunk(t, b, c, reuse=True):
                if c == 0:
                    dve.wait_ge(adj_loaded[b], (t + NT + 2 - b) * 8)
                    if reuse:
                        dve.wait_ge(exp_done, t)
                wait_apart(dve, dve_value, qk_done, t * NG + c + 1, x_split_done)
                cs = slice(c * BANK, (c + 1) * BANK)
                nc.vector.tensor_tensor_reduce(score[:, cs], ps_s[c % 2][:, :], adj_s[b][:, cs], 1.0, -3.0e38,
                                               ALU.add, ALU.max, chunk_max[:, c:c + 1]).then_inc(score_done, 1)
                if c == NG - 1:
                    dve.wait_ge(score_done, t * NG + NG)
                    dve.sem_inc(adj_used, 1)

            def softmax_bias(t):
                nc.vector.tensor_reduce(row_max[:, :], chunk_max[:, :], AX.X, ALU.max).then_inc(row_max_done, 1)
                dve.wait_ge(row_max_done, t + 1)
                nc.vector.scalar_tensor_tensor(out=top[:, :], in0=row_max[:, :], scalar=2.0,
                                               in1=c_row[:, bass.ds(t, 1)], op0=ALU.mult,
                                               op1=ALU.add).then_inc(top_done, 1)
                dve.wait_ge(top_done, t + 1)
                nc.vector.scalar_tensor_tensor(out=exp_bias[:, :], in0=c_row[:, bass.ds(t, 1)], scalar=P_SHIFT,
                                               in1=top[:, :], op0=ALU.add, op1=ALU.subtract).then_inc(bias_done, 1)

            def attend(t, b):
                dve.wait_ge(exp_done, t + 1)
                nc.vector.reciprocal(den_r[:, :], den[b][:, :]).then_inc(den_r_done, 1)
                dve.wait_ge(den_r_done, t + 1)
                residual(t + NT, xs[:, bass.ds(t, 1), :], b, den_r[:, :], t)

            def out_tile(t, b, reuse=True):
                if reuse:
                    dve.wait_ge(out_stored[b], (t - b) * 8)
                normalise(t + NT, out_t[b][:, :], out_ready)

            def y_lo_tile(t, b):
                dve.wait_ge(y_hi_done, t + 1)
                nc.vector.tensor_tensor(yt_lo[b][:, :, :], y_f[:, :, :], yt_hi[b][:, :, :],
                                        ALU.subtract).then_inc(y_lo_done, 1)

            def layer2_step(t, b, qk=True, pv=True, z=True, y=True, reuse=True):
                if z:
                    attend(t - 2, b)
                for c in range(NG):
                    if qk:
                        score_chunk(t, b, c, reuse=pv)
                    if pv:
                        lo_group((t + (NT - 1)) * NG + c, 1 - b, c)
                    if z and c == 1:
                        out_tile(t - 2, b, reuse)
                if qk:
                    softmax_bias(t)
                if y:
                    y_lo_tile(t + 1, 1 - b)

            dve.wait_ge(x1_kept, NT)
            y_lo_tile(0, 0)
            layer2_step(0, 0, pv=False, z=False)
            layer2_step(1, 1, z=False)
            layer2_step(2, 0, reuse=False)
            layer2_step(3, 1, reuse=False)
            with dve.Fori(4, NT - 3, 2) as t:
                for b in range(2):
                    layer2_step(t + b, b)
            layer2_step(NT - 2, 0)
            layer2_step(NT - 1, 1, y=False)
            layer2_step(NT, 0, qk=False, y=False)
            layer2_step(NT + 1, 1, qk=False, pv=False, y=False)


def kernel(x, adj, L1_gnn_Wq, L1_gnn_bq, L1_gnn_Wk, L1_gnn_bk, L1_gnn_Wv, L1_gnn_bv):
    import concourse.bacc as bacc
    from concourse.bass_utils import run_bass_kernel_spmd

    def blocks(b):
        return np.ascontiguousarray(np.asarray(b).reshape(-1, P).T)

    nc = bacc.Bacc("TRN2", target_bir_lowering=False, num_devices=1)
    arrays = {
        "x": np.ascontiguousarray(x),
        "adj": np.ascontiguousarray(adj),
        "wq": np.ascontiguousarray(L1_gnn_Wq),
        "wk": np.ascontiguousarray(L1_gnn_Wk),
        "wv_t": np.ascontiguousarray(np.asarray(L1_gnn_Wv).T),
        "bq": blocks(L1_gnn_bq),
        "bk": blocks(L1_gnn_bk),
        "bv": np.ascontiguousarray(np.broadcast_to(np.asarray(L1_gnn_bv), (P, L1_gnn_bv.shape[0]))),
    }
    args = [nc.dram_tensor(f"in_{k}", a.shape, mybir.dt.from_np(a.dtype), kind="ExternalInput").ap()
            for k, a in arrays.items()]
    out = nc.dram_tensor("out", arrays["x"].shape, F32, kind="ExternalOutput").ap()
    gnn_layers(nc, *args, out)
    result = run_bass_kernel_spmd(nc, [{f"in_{k}": a for k, a in arrays.items()}], core_ids=[0])
    return result.results[0]["out"]
```

```python
from contextlib import ExitStack

import numpy as np

import concourse.bass as bass
from concourse import mybir

F32 = mybir.dt.float32
F16 = mybir.dt.float16
BF16 = mybir.dt.bfloat16
ALU = mybir.AluOpType
ACT = mybir.ActivationFunctionType
AX = mybir.AxisListType

P = 128
LANES = 4
BANK = LANES * P

X_SCALE = 1.0 / 8
W_SCALE = 16.0
Y_SCALE = 1.0 / 4
P_SHIFT = 12 * float(np.log(2.0))
LN_EPS = 1e-5
HEAD_EPS = 1e-12


def gnn_layers(nc, x, adj, wq, wk, wv_t, bq, bk, bv, out):
    N, D = x.shape
    NT = N // P
    KD = D // P
    NG = N // BANK
    HALF = N // 2
    RING = 4
    DEG_SCALE = 1.0 / (2.0 * float(np.sqrt(D)))
    assert N % BANK == 0 and KD == 2 and NT % RING == 0 and NT >= 10
    assert X_SCALE * Y_SCALE == DEG_SCALE

    with ExitStack() as ctx:
        def sb(name, shape, dt=F32):
            return ctx.enter_context(nc.sbuf_tensor(name, shape, dt))

        def ps(name, shape, dt=F32):
            return ctx.enter_context(nc.psum_tensor(name, shape, dt))

        def sem(name):
            return ctx.enter_context(nc.semaphore(name))

        ident = sb("ident", [P, P])
        ones = sb("ones", [P, P])
        minus_half = sb("minus_half", [P, 1])
        xs = sb("xs", [P, NT, D])
        x_split = sb("x_split", [P, NT, 2 * D], F16)
        wq_s = sb("wq_s", [P, KD, D])
        wk_s = sb("wk_s", [P, KD, D])
        wv_s = sb("wv_s", [P, KD, D])
        bq_s = sb("bq_s", [P, KD])
        bk_s = sb("bk_s", [P, KD])
        bv_s = sb("bv_s", [P, D])
        bq_wide = sb("bq_wide", [P, KD, P])
        g_hi = sb("g_hi", [P, KD, D], F16)
        g_lo = sb("g_lo", [P, KD, D], F16)
        y_bias = sb("y_bias", [P, KD])
        wv_u = sb("wv_u", [P, KD, D + 2])
        wv_hi = sb("wv_hi", [P, KD, D + 2], F16)
        wv_lo = sb("wv_lo", [P, KD, D + 2], F16)
        c_bias = sb("c_bias", [P, 1])

        adj_s = sb("adj_s", [P, RING, N])
        score = adj_s[:, RING - 2, :]
        prob = adj_s[:, RING - 1, :]
        sign = sb("sign", [P, N], BF16)
        mask = sb("mask", [P, N], BF16)
        inc = [sb(f"inc{i}", [P, N]) for i in range(2)]
        count = sb("count", [P, 2])
        head_r = sb("head_r", [P, 2])
        t_hi = [sb(f"t_hi{i}", [P, NT, P], F16) for i in range(2)]
        t_lo = [sb(f"t_lo{i}", [P, NT, P], F16) for i in range(2)]
        deg = sb("deg", [P, 1])
        deg_parts = sb("deg_parts", [P, 2])
        deg_r = sb("deg_r", [P, NT])
        z = sb("z", [P, D])
        stats = sb("stats", [P, 6])
        mv = sb("mv", [P, 2])
        var_eps = sb("var_eps", [P, 1])
        rstd = sb("rstd", [P, 1])
        x1_t = [sb(f"x1_t{i}", [P, D]) for i in range(2)]
        xt_hi = sb("xt_hi", [P, KD, N], F16)
        xt_lo = sb("xt_lo", [P, KD, N], F16)
        v_split = sb("v_split", [P, NT, 2 * D], F16)
        c_row = sb("c_row", [P, NT])
        y_t = sb("y_t", [P, KD, N])
        yt_hi = [sb(f"yt_hi{i}", [P, KD, P], F16) for i in range(2)]
        yt_lo = [sb(f"yt_lo{i}", [P, KD, P], F16) for i in range(2)]
        chunk_max = sb("chunk_max", [P, NG])
        row_max = sb("row_max", [P, 1])
        top = sb("top", [P, 1])
        exp_bias = sb("exp_bias", [P, 1])
        den = sb("den", [P, 1])
        den_r = sb("den_r", [P, NT])
        out_t = [sb(f"out_t{i}", [P, D]) for i in range(2)]

        ps_o = [ps(f"ps_o{i}", [P, BANK]) for i in range(2)]
        ps_s = [ps(f"ps_s{i}", [P, BANK]) for i in range(NG)]
        ps_t = [ps(f"ps_t{i}", [P, BANK]) for i in range(2)]
        ps_xt, ps_v = ps_t
        ps_y = ps_xt
        ps_w, ps_b = ps_t

        adj_loaded = [sem(f"adj_loaded{i}") for i in range(2)]
        adj_half_loaded = sem("adj_half_loaded")
        x_loaded = [sem(f"x_loaded{i}") for i in range(NG)]
        w_loaded = sem("w_loaded")
        const_ready = sem("const_ready")
        ident_ready = sem("ident_ready")
        x_hi_done = sem("x_hi_done")
        x_split_done = sem("x_split_done")
        bq_wide_done = sem("bq_wide_done")
        g_done = sem("g_done")
        g_hi_done = sem("g_hi_done")
        g_split_done = sem("g_split_done")
        w_bias_done = sem("w_bias_done")
        wv_u_done = sem("wv_u_done")
        wv_hi_done = sem("wv_hi_done")
        sign_done = sem("sign_done")
        mask0_done = sem("mask0_done")
        count_done = sem("count_done")
        head_floor = sem("head_floor")
        head_done = sem("head_done")
        inc0_done = sem("inc0_done")
        inc_done = sem("inc_done")
        trans_done = sem("trans_done")
        hi_done = sem("hi_done")
        lo_done = sem("lo_done")
        prod_done = sem("prod_done")
        deg_done = sem("deg_done")
        deg_r_done = sem("deg_r_done")
        z_done = sem("z_done")
        stats_done = sem("stats_done")
        mv_done = sem("mv_done")
        var_done = sem("var_done")
        rstd_done = sem("rstd_done")
        x1_done = sem("x1_done")
        x1_kept = sem("x1_kept")
        xt_done = sem("xt_done")
        xt_hi_done = sem("xt_hi_done")
        xt_lo_done = sem("xt_lo_done")
        v_done = sem("v_done")
        v_hi_done = sem("v_hi_done")
        v_lo_done = sem("v_lo_done")
        y_done = sem("y_done")
        y_kept = sem("y_kept")
        y_hi_done = sem("y_hi_done")
        y_lo_done = sem("y_lo_done")
        qk_done = sem("qk_done")
        score_done = sem("score_done")
        row_max_done = sem("row_max_done")
        top_done = sem("top_done")
        bias_done = sem("bias_done")
        exp_done = sem("exp_done")
        den_r_done = sem("den_r_done")
        out_ready = sem("out_ready")
        out_stored = [sem(f"out_stored{i}") for i in range(2)]

        adj_rows = adj.rearrange("(t p) n -> t p n", p=P)
        out_rows = out.rearrange("(t p) d -> t p d", p=P)
        x_rows = x.rearrange("(t p) d -> p t d", p=P)
        XT = NT // NG

        def dma_count(n, b):
            return (n + 2 - b) * 8

        def wait_apart(eng, settled, *awaited):
            for reg, _, value in awaited:
                eng.reg_mov(reg, value)
            eng.wait_ge(settled, 1)
            for reg, semaphore, _ in awaited:
                eng.wait_ge(semaphore, reg)

        block = ctx.enter_context(nc.Block())

        @block.sync
        def _(sp):
            def load_adj1(n, slot):
                if not isinstance(n, int) or n >= RING:
                    sp.wait_ge(count_done, n - 1)
                sp.dma_start(adj_s[:, slot, :], adj_rows[n, :, :]).then_inc(adj_loaded[slot % 2], 16)

            def load_adj2(t, b, first=False):
                if first:
                    sp.wait_ge(count_done, NT + t - 1)
                else:
                    sp.wait_ge(score_done, (t - 1) * NG)
                sp.dma_start(adj_s[:, b, :], adj_rows[t, :, :]).then_inc(adj_loaded[b], 16)

            def store_out(t, b):
                sp.wait_ge(out_ready, t + 1)
                sp.dma_start(out_rows[t, :, :], out_t[b][:, :]).then_inc(out_stored[b], 16)

            sp.dma_start(adj_s[:, 0, 0:HALF], adj_rows[0, :, 0:HALF]).then_inc(adj_half_loaded, 16)
            sp.dma_start(adj_s[:, 0, HALF:N], adj_rows[0, :, HALF:N]).then_inc(adj_loaded[0], 16)
            load_adj1(1, 1)
            sp.wait_ge(adj_loaded[0], 16)
            load_adj1(2, 2)
            sp.wait_ge(adj_loaded[1], 16)
            load_adj1(3, 3)
            with sp.Fori(RING, NT - RING + 1, RING) as n:
                for slot in range(RING):
                    load_adj1(n + slot, slot)
            for b in range(2):
                load_adj2(b, b, first=True)
            load_adj2(2, 0)
            load_adj2(3, 1)
            with sp.Fori(2, NT - 3, 2) as t:
                for b in range(2):
                    load_adj2(t + b + 2, b)
                    store_out(t + b - 2, b)
            for t in range(NT - 4, NT):
                store_out(t, t % 2)
            for b in range(2):
                sp.wait_ge(out_stored[b], 16 * (NT // 2))

        @block.gpsimd
        def _(pool):
            pool_value = pool.alloc_register("pool_value")
            nc.gpsimd.memset(minus_half[:, :], -0.5).then_inc(const_ready, 1)
            nc.gpsimd.memset(ones[:, :], 1.0).then_inc(const_ready, 1)
            nc.gpsimd.memset(ident[:, :], 0.0).then_inc(const_ready, 1)
            pool.wait_ge(const_ready, 3)
            nc.gpsimd.affine_select(out=ident[:, :], in_=ident[:, :], compare_op=ALU.not_equal, fill=1.0,
                                    base=0, pattern=[[-1, P]], channel_multiplier=1).then_inc(ident_ready, 1)

            def head_norm(n, b):
                wait_apart(pool, const_ready, (pool_value, count_done, n + 1))
                nc.gpsimd.tensor_scalar(head_r[:, b:b + 1], count[:, b:b + 1], HEAD_EPS ** 2, None,
                                        ALU.max).then_inc(head_floor, 1)
                pool.wait_ge(head_floor, n + 1)
                nc.gpsimd.tensor_tensor(head_r[:, b:b + 1], head_r[:, b:b + 1], minus_half[:, :],
                                        ALU.pow).then_inc(head_done, 1)

            def row_rstd(n):
                pool.wait_ge(var_done, n + 1)
                nc.gpsimd.tensor_tensor(rstd[:, :], var_eps[:, :], minus_half[:, :],
                                        ALU.pow).then_inc(rstd_done, 1)

            def keep_x1(t, b):
                pool.wait_ge(x1_done, t + 1)
                nc.gpsimd.tensor_tensor(xs[:, bass.ds(t, 1), :], x1_t[b][:, :], bv_s[:, :],
                                        ALU.add).then_inc(x1_kept, 1)

            for n in range(3):
                head_norm(n, n % 2)
            pool.wait_ge(w_loaded, 16 * 6)
            pool.wait_ge(x_split_done, NG)
            with pool.Fori(0, NT - 5, 2) as t:
                for b in range(2):
                    head_norm(t + b + 3, 1 - b)
                    row_rstd(t + b)
                    keep_x1(t + b, b)
            head_norm(NT - 1, 1)
            for t in range(NT - 4, NT):
                row_rstd(t)
                keep_x1(t, t % 2)
            with pool.Fori(0, NT) as t:
                row_rstd(t + NT)

        @block.tensor
        def _(pe):
            def weights():
                pe.wait_ge(w_loaded, 16 * 6)
                pe.wait_ge(bq_wide_done, KD)
                for m in range(KD):
                    for k in range(KD):
                        nc.tensor.matmul(ps_w[:, m * D:(m + 1) * D], wq_s[:, k, m * P:(m + 1) * P],
                                         wk_s[:, k, :], start=(k == 0), stop=(k == KD - 1))
                for m in range(KD):
                    for k in range(KD):
                        nc.tensor.matmul(ps_b[:, m:m + 1], wk_s[:, k, m * P:(m + 1) * P], bq_s[:, k:k + 1],
                                         start=(k == 0), stop=(k == KD - 1))
                for m in range(KD):
                    for k in range(KD):
                        nc.tensor.matmul(ps_b[:, KD + m:KD + m + 1], wq_s[:, k, m * P:(m + 1) * P],
                                         bk_s[:, k:k + 1], start=(k == 0), stop=(k == KD - 1))
                for k in range(KD):
                    last = nc.tensor.matmul(ps_b[:, 2 * KD:2 * KD + 1], bq_wide[:, k, :], bk_s[:, k:k + 1],
                                            start=(k == 0), stop=(k == KD - 1))
                last.then_inc(g_done, 1)

            def transpose_group(src, g, bank):
                for i in range(LANES):
                    c = (g * LANES + i) * P
                    last = nc.tensor.transpose(bank[:, i * P:(i + 1) * P], src[:, c:c + P], ident[:, :])
                last.then_inc(trans_done, 1)

            def product_group(b, g, right):
                for j in range(g * LANES, (g + 1) * LANES):
                    for a, (left, c) in enumerate(((t_hi[b], 0), (t_hi[b], D), (t_lo[b], 0))):
                        last = nc.tensor.matmul(ps_o[b][:, 0:D], left[:, j, :], right[:, j, c:c + D],
                                                start=(j == 0 and a == 0), stop=(j == NT - 1 and a == 2))
                if g == NG - 1:
                    last.then_inc(prod_done, 1)

            def x1_transpose(t, b, first=False):
                pe.wait_ge(x1_done, t + 1)
                if first:
                    pe.wait_ge(g_split_done, KD)
                else:
                    pe.wait_ge(y_kept, t * KD)
                for k in range(KD):
                    last = nc.tensor.transpose(ps_xt[:, k * P:(k + 1) * P], x1_t[b][:, k * P:(k + 1) * P],
                                               ident[:, :])
                last.then_inc(xt_done, 1)

            def v_y_product(t, first=False):
                pe.wait_ge(xt_lo_done, t + 1)
                if not first:
                    pe.wait_ge(v_lo_done, t)
                xh = [xt_hi[:, k, bass.ts(t, P)] for k in range(KD)]
                xl = [xt_lo[:, k, bass.ts(t, P)] for k in range(KD)]
                for k in range(KD):
                    for a, (left, right) in enumerate(((xh, wv_hi), (xh, wv_lo), (xl, wv_hi))):
                        last = nc.tensor.matmul(ps_v[:, 0:D + 2], left[k], right[:, k, :],
                                                start=(k == 0 and a == 0), stop=(k == KD - 1 and a == 2))
                last.then_inc(v_done, 1)
                for m in range(KD):
                    gs = slice(m * P, (m + 1) * P)
                    for k in range(KD):
                        for a, (left, right) in enumerate(((g_hi, xh), (g_hi, xl), (g_lo, xh))):
                            last = nc.tensor.matmul(ps_y[:, gs], left[:, k, gs], right[k],
                                                    start=(k == 0 and a == 0), stop=(k == KD - 1 and a == 2))
                last.then_inc(y_done, 1)

            def layer1_step(t, b, trans=True, prod=True, vy=True, xt=True, first=False):
                for g in range(NG):
                    if trans:
                        if g == 0:
                            pe.wait_ge(inc_done, t + 1)
                        if not first:
                            pe.wait_ge(lo_done, t * NG + (g + 1 - NG))
                        transpose_group(inc[b], g, ps_s[g])
                    if prod:
                        if g == 0 and xt:
                            pe.wait_ge(z_done, t - 1)
                        pe.wait_ge(lo_done, t * NG + (g + 1 - NG))
                        product_group(1 - b, g, x_split)
                    if g == 0 and vy:
                        v_y_product(t - 3, first=(vy == "first"))
                if xt:
                    x1_transpose(t - 2, b, first=(vy is False))

            pe.wait_ge(ident_ready, 1)
            for g in range(NG):
                if g % 2 == 0:
                    pe.wait_ge(inc0_done, g // 2 + 1)
                transpose_group(inc[0], g, ps_s[g])
            for g in range(NG):
                pe.wait_ge(x_split_done, g + 1)
                pe.wait_ge(lo_done, g + 1)
                product_group(0, g, x_split)
            pe.wait_ge(inc_done, 2)
            for g in range(NG):
                transpose_group(inc[1], g, ps_s[g])
            weights()
            layer1_step(2, 0, vy=False)
            pe.wait_ge(wv_hi_done, 2)
            layer1_step(3, 1, vy="first")
            with pe.Fori(4, NT - 1, 2) as t:
                for b in range(2):
                    layer1_step(t + b, b)
            layer1_step(NT, 0, trans=False)

            def qk_chunk(t, b, c, first):
                if c == 0:
                    pe.wait_ge(y_lo_done, t + 1)
                if not first:
                    pe.wait_ge(score_done, t * NG + (c + 1 - NG))
                cs = slice(c * BANK, (c + 1) * BANK)
                for k in range(KD):
                    for a, (left, right) in enumerate(((yt_hi[b], xt_hi), (yt_hi[b], xt_lo), (yt_lo[b], xt_hi))):
                        last = nc.tensor.matmul(ps_s[c][:, :], left[:, k, :], right[:, k, cs],
                                                start=(k == 0 and a == 0), stop=(k == KD - 1 and a == 2))
                last.then_inc(qk_done, 1)

            def layer2_step(t, b, qk=True, first=False):
                for c in range(NG):
                    if qk:
                        qk_chunk(t, b, c, first=False)
                    if c == 0:
                        pe.wait_ge(exp_done, t)
                    if not (first and c < 2):
                        pe.wait_ge(lo_done, (t + (NT - 1)) * NG + (c - 1))
                    transpose_group(prob, c, ps_t[c % 2])
                pe.wait_ge(z_done, t + (NT - 2))
                for g in range(NG):
                    pe.wait_ge(lo_done, (t + (NT - 1)) * NG + g + 1)
                    product_group(1 - b, g, v_split)

            v_y_product(NT - 2)
            pe.wait_ge(lo_done, NT * NG)
            for c in range(NG - 1):
                qk_chunk(0, 0, c, first=True)
            x1_transpose(NT - 1, 1)
            v_y_product(NT - 1)
            qk_chunk(0, 0, NG - 1, first=True)
            pe.wait_ge(y_kept, NT * KD)
            pe.wait_ge(v_lo_done, NT)
            layer2_step(1, 1, first=True)
            with pe.Fori(2, NT - 1, 2) as t:
                for b in range(2):
                    layer2_step(t + b, b)
            layer2_step(NT, 0, qk=False)

        @block.scalar
        def _(act):
            for g in range(NG):
                ts = slice(g * XT, (g + 1) * XT)
                act.dma_start(xs[:, ts, :], x_rows[:, ts, :]).then_inc(x_loaded[g], 16)
            act.dma_start(bq_s[:, :], bq).then_inc(w_loaded, 16)
            act.dma_start(bk_s[:, :], bk).then_inc(w_loaded, 16)
            act.dma_start(bv_s[:, :], bv).then_inc(w_loaded, 16)
            for name, src in ((wq_s, wq), (wk_s, wk), (wv_s, wv_t)):
                act.dma_start(name[:, :, :], src.rearrange("(k p) d -> p k d", p=P)).then_inc(w_loaded, 16)

            def sign_tile(n, b):
                act.wait_ge(adj_loaded[b], dma_count(n, b))
                if not isinstance(n, int) or n >= 2:
                    act.wait_ge(count_done, n)
                nc.scalar.activation(sign[:, :], adj_s[:, bass.ds(n % RING, 1), :], ACT.Sign).then_inc(sign_done, 1)

            def mask_tile(n, b):
                act.wait_ge(inc_done, n)
                act.wait_ge(sign_done, n)
                nc.scalar.activation(mask[:, :], sign[:, :], ACT.Relu,
                                     accum_out=count[:, b:b + 1]).then_inc(count_done, 1)

            def hi_group(n, b, g, bank):
                act.wait_ge(trans_done, n + 1)
                nc.scalar.copy(t_hi[b][:, g * LANES:(g + 1) * LANES, :], bank[:, :]).then_inc(hi_done, 1)

            def xt_hi_tile(t):
                act.wait_ge(xt_done, t + 1)
                nc.scalar.activation(xt_hi[:, :, bass.ts(t, P)],
                                     ps_xt[:, 0:KD * P].rearrange("p (k n) -> p k n", k=KD),
                                     ACT.Copy, scale=X_SCALE).then_inc(xt_hi_done, 1)

            def v_y_tile(t):
                act.wait_ge(v_done, t + 1)
                nc.scalar.activation(c_row[:, bass.ds(t, 1)], ps_v[:, D:D + 1], ACT.Identity,
                                     scale=2 * DEG_SCALE / (X_SCALE * W_SCALE), bias=c_bias[:, :])
                nc.scalar.activation(v_split[:, bass.ds(t, 1), 0:D], ps_v[:, 0:D], ACT.Copy,
                                     scale=1.0 / (X_SCALE * W_SCALE)).then_inc(v_hi_done, 1)
                act.wait_ge(y_done, t + 1)
                for m in range(KD):
                    nc.scalar.activation(y_t[:, m, bass.ts(t, P)], ps_y[:, m * P:(m + 1) * P], ACT.Identity,
                                         scale=Y_SCALE / (X_SCALE * W_SCALE),
                                         bias=y_bias[:, m:m + 1]).then_inc(y_kept, 1)

            def x_hi_part(g):
                ts = slice(g * XT, (g + 1) * XT)
                act.wait_ge(x_loaded[g], 16)
                nc.scalar.copy(x_split[:, ts, 0:D], xs[:, ts, :]).then_inc(x_hi_done, 1)

            def layer1_step(t, b, trans=True, ahead=True, xt=True, reuse=True):
                if xt:
                    xt_hi_tile(t - 3)
                if trans and reuse:
                    act.wait_ge(prod_done, t - 1)
                for g in range(NG):
                    if trans:
                        hi_group(t * NG + g, b, g, ps_s[g])
                    if g == 0 and xt:
                        v_y_tile(t - 3)
                    if g == 1 and ahead:
                        sign_tile(t + 2, b)
                    if g == 2 and ahead:
                        mask_tile(t + 2, b)

            x_hi_part(0)
            x_hi_part(1)
            sign_tile(1, 1)
            for g in range(NG):
                hi_group(g, 0, g, ps_s[g])
                if g == 1:
                    mask_tile(1, 1)
                    x_hi_part(2)
            x_hi_part(3)
            sign_tile(2, 0)
            mask_tile(2, 0)
            layer1_step(1, 1, xt=False, reuse=False)
            act.wait_ge(g_done, 1)
            for m in range(KD):
                nc.scalar.activation(g_hi[:, m, :], ps_w[:, m * D:(m + 1) * D], ACT.Copy,
                                     scale=W_SCALE).then_inc(g_hi_done, 1)
            act.wait_ge(wv_u_done, 2 * KD)
            nc.scalar.copy(wv_hi[:, :, :], wv_u[:, :, :]).then_inc(wv_hi_done, 1)
            act.wait_ge(w_bias_done, 2)
            layer1_step(2, 0, xt=False)
            layer1_step(3, 1)
            with act.Fori(4, NT - 3, 2) as t:
                for b in range(2):
                    layer1_step(t + b, b)
            layer1_step(NT - 2, 0, ahead=False)
            layer1_step(NT - 1, 1, ahead=False)
            layer1_step(NT, 0, trans=False, ahead=False)

            def y_hi_tile(t, b):
                nc.scalar.copy(yt_hi[b][:, :, :], y_t[:, :, bass.ts(t, P)]).then_inc(y_hi_done, 1)

            def layer2_step(t, b, pv=True, y=True):
                if y:
                    act.wait_ge(qk_done, t * NG)
                    y_hi_tile(t + 1, 1 - b)
                if pv:
                    for g in range(NG):
                        hi_group((t + (NT - 1)) * NG + g, 1 - b, g, ps_t[g % 2])
                    act.wait_ge(den_r_done, t)
                act.wait_ge(bias_done, t + 1)
                nc.scalar.activation(prob, score, ACT.Exp, scale=2.0, bias=exp_bias[:, :],
                                     accum_out=den[:, :]).then_inc(exp_done, 1)

            act.wait_ge(y_kept, 2 * KD)
            y_hi_tile(0, 0)
            y_hi_tile(1, 1)
            xt_hi_tile(NT - 2)
            v_y_tile(NT - 2)
            xt_hi_tile(NT - 1)
            v_y_tile(NT - 1)
            act.wait_ge(y_kept, NT * KD)
            layer2_step(0, 0, pv=False, y=False)
            with act.Fori(1, NT - 2, 2) as t:
                for b in range(2):
                    layer2_step(t + b, 1 - b)
            layer2_step(NT - 1, 1, y=False)
            for g in range(NG):
                hi_group((2 * NT - 1) * NG + g, 1, g, ps_t[g % 2])

        @block.vector
        def _(dve):
            dve_value = dve.alloc_register("dve_value")

            def inc_tile(n, b):
                dve.wait_ge(head_done, n + 1)
                if not isinstance(n, int) or n >= 2:
                    dve.wait_ge(trans_done, (n - 1) * NG)
                dve.wait_ge(deg_r_done, n)
                nc.vector.scalar_tensor_tensor(
                    out=inc[b][:, :], in0=mask[:, :], scalar=head_r[:, b:b + 1],
                    in1=adj_s[:, bass.ds(n % RING, 1), :],
                    op0=ALU.mult, op1=ALU.add, accum_out=deg[:, :]).then_inc(inc_done, 1)
                dve.wait_ge(inc_done, n + 1)
                nc.vector.reciprocal(deg_r[:, bass.ds(n, 1)], deg[:, :]).then_inc(deg_r_done, 1)

            def lo_group(n, b, g, bank):
                dve.wait_ge(hi_done, n + 1)
                nc.vector.tensor_tensor(t_lo[b][:, g * LANES:(g + 1) * LANES, :],
                                        bank[:, :].rearrange("p (a n) -> p a n", a=LANES),
                                        t_hi[b][:, g * LANES:(g + 1) * LANES, :],
                                        ALU.subtract).then_inc(lo_done, 1)

            def residual(n, base, b, scale):
                dve.wait_ge(prod_done, n + 1)
                nc.vector.scalar_tensor_tensor(out=z[:, :], in0=ps_o[b][:, 0:D], scalar=scale,
                                               in1=base, op0=ALU.mult, op1=ALU.add).then_inc(z_done, 1)
                dve.wait_ge(z_done, n + 1)
                nc.vector.bn_stats(stats[:, :], z[:, :]).then_inc(stats_done, 1)
                wait_apart(dve, const_ready, (dve_value, stats_done, n + 1))
                nc.vector.bn_aggr(mv[:, :], stats[:, :]).then_inc(mv_done, 1)
                dve.wait_ge(mv_done, n + 1)
                nc.vector.tensor_scalar(var_eps[:, :], mv[:, 1:2], LN_EPS, None, ALU.add).then_inc(var_done, 1)

            def normalise(n, dst, done):
                dve.wait_ge(rstd_done, n + 1)
                nc.vector.tensor_scalar(dst, z[:, :], mv[:, 0:1], rstd[:, :], ALU.subtract,
                                        ALU.mult).then_inc(done, 1)

            def edge(t, b):
                dve.wait_ge(deg_r_done, t + 1)
                if not isinstance(t, int) or t > 0:
                    dve.wait_ge(x1_done, t)
                residual(t, xs[:, bass.ds(t, 1), :], b, deg_r[:, bass.ds(t, 1)])

            def x1_tile(t, b, reuse=True):
                if reuse:
                    dve.wait_ge(xt_done, t - 1)
                    dve.wait_ge(x1_kept, t - 1)
                normalise(t, x1_t[b][:, :], x1_done)

            def xt_lo_tile(t):
                dve.wait_ge(xt_hi_done, t + 1)
                nc.vector.scalar_tensor_tensor(out=xt_lo[:, :, bass.ts(t, P)],
                                               in0=ps_xt[:, 0:KD * P].rearrange("p (k n) -> p k n", k=KD),
                                               scalar=X_SCALE, in1=xt_hi[:, :, bass.ts(t, P)],
                                               op0=ALU.mult, op1=ALU.subtract).then_inc(xt_lo_done, 1)

            def v_lo_tile(t):
                dve.wait_ge(v_hi_done, t + 1)
                nc.vector.scalar_tensor_tensor(out=v_split[:, bass.ds(t, 1), D:2 * D], in0=ps_v[:, 0:D],
                                               scalar=1.0 / (X_SCALE * W_SCALE),
                                               in1=v_split[:, bass.ds(t, 1), 0:D],
                                               op0=ALU.mult, op1=ALU.subtract).then_inc(v_lo_done, 1)

            def layer1_step(t, b, trans=True, ahead=True, z=True, xt=True, reuse=True):
                if xt:
                    xt_lo_tile(t - 3)
                if z:
                    edge(t - 2, b)
                if trans:
                    lo_group(t * NG, b, 0, ps_s[0])
                if ahead:
                    inc_tile(t + 1, 1 - b)
                if z:
                    x1_tile(t - 2, b, reuse)
                if trans:
                    lo_group(t * NG + 1, b, 1, ps_s[1])
                if xt:
                    v_lo_tile(t - 3)
                if trans:
                    lo_group(t * NG + 2, b, 2, ps_s[2])
                    lo_group(t * NG + 3, b, 3, ps_s[3])

            dve.wait_ge(adj_half_loaded, 16)
            nc.vector.tensor_scalar(mask[:, 0:HALF], adj_s[:, 0, 0:HALF], 0.0, 0.0, ALU.is_gt, ALU.add,
                                    accum_out=deg_parts[:, 0:1]).then_inc(mask0_done, 1)
            dve.wait_ge(adj_loaded[0], 16)
            nc.vector.tensor_scalar(mask[:, HALF:N], adj_s[:, 0, HALF:N], 0.0, 0.0, ALU.is_gt, ALU.add,
                                    accum_out=deg_parts[:, 1:2]).then_inc(mask0_done, 1)
            dve.wait_ge(mask0_done, 2)
            nc.vector.tensor_tensor(count[:, 0:1], deg_parts[:, 0:1], deg_parts[:, 1:2],
                                    ALU.add).then_inc(count_done, 1)

            def x_lo_part(g):
                ts = slice(g * XT, (g + 1) * XT)
                dve.wait_ge(x_hi_done, g + 1)
                nc.vector.tensor_tensor(x_split[:, ts, D:2 * D], xs[:, ts, :], x_split[:, ts, 0:D],
                                        ALU.subtract).then_inc(x_split_done, 1)

            dve.wait_ge(head_done, 1)
            for h in range(2):
                hs = slice(h * HALF, (h + 1) * HALF)
                nc.vector.scalar_tensor_tensor(
                    out=inc[0][:, hs], in0=mask[:, hs], scalar=head_r[:, 0:1], in1=adj_s[:, 0, hs],
                    op0=ALU.mult, op1=ALU.add, accum_out=deg_parts[:, h:h + 1]).then_inc(inc0_done, 1)
            dve.wait_ge(inc0_done, 2)
            nc.vector.tensor_tensor(deg[:, :], deg_parts[:, 0:1], deg_parts[:, 1:2],
                                    ALU.add).then_inc(deg_done, 1)
            dve.sem_inc(inc_done, 1)
            dve.wait_ge(deg_done, 1)
            nc.vector.reciprocal(deg_r[:, 0:1], deg[:, :]).then_inc(deg_r_done, 1)
            for g in range(2):
                x_lo_part(g)
                lo_group(g, 0, g, ps_s[g])
            for g in range(2, NG):
                lo_group(g, 0, g, ps_s[g])
                x_lo_part(g)
            inc_tile(1, 1)
            dve.wait_ge(w_loaded, 16 * 6)
            dve.wait_ge(const_ready, 2)
            for k in range(KD):
                nc.vector.tensor_scalar(bq_wide[:, k, :], ones[:, :], bq_s[:, k:k + 1], None,
                                        ALU.mult).then_inc(bq_wide_done, 1)
                nc.vector.tensor_scalar(wv_u[:, k, 0:D], wv_s[:, k, :], W_SCALE, None,
                                        ALU.mult).then_inc(wv_u_done, 1)
            layer1_step(1, 1, z=False, xt=False)
            dve.wait_ge(g_done, 1)
            nc.vector.tensor_scalar(y_bias[:, :], ps_b[:, 0:KD], Y_SCALE, None, ALU.mult).then_inc(w_bias_done, 1)
            nc.vector.tensor_scalar(c_bias[:, :], ps_b[:, 2 * KD:2 * KD + 1], 2 * DEG_SCALE, None,
                                    ALU.mult).then_inc(w_bias_done, 1)
            for k in range(KD):
                nc.vector.tensor_scalar(wv_u[:, k, D:D + 2], ps_b[:, KD + k:KD + k + 1].to_broadcast([P, 2]),
                                        W_SCALE, None, ALU.mult).then_inc(wv_u_done, 1)
            dve.wait_ge(g_hi_done, KD)
            for m in range(KD):
                nc.vector.scalar_tensor_tensor(out=g_lo[:, m, :], in0=ps_w[:, m * D:(m + 1) * D], scalar=W_SCALE,
                                               in1=g_hi[:, m, :], op0=ALU.mult,
                                               op1=ALU.subtract).then_inc(g_split_done, 1)
            dve.wait_ge(wv_hi_done, 1)
            nc.vector.tensor_tensor(wv_lo[:, :, :], wv_u[:, :, :], wv_hi[:, :, :], ALU.subtract).then_inc(wv_hi_done, 1)
            layer1_step(2, 0, xt=False, reuse=False)
            layer1_step(3, 1, reuse=False)
            with dve.Fori(4, NT - 3, 2) as t:
                for b in range(2):
                    layer1_step(t + b, b)
            layer1_step(NT - 2, 0)
            layer1_step(NT - 1, 1, ahead=False)
            layer1_step(NT, 0, trans=False, ahead=False)

            def score_chunk(t, b, c):
                if c == 0:
                    dve.wait_ge(adj_loaded[b], dma_count(t + NT, b))
                    if not isinstance(t, int) or t > 0:
                        dve.wait_ge(exp_done, t)
                wait_apart(dve, x_split_done, (dve_value, qk_done, t * NG + c + 1))
                cs = slice(c * BANK, (c + 1) * BANK)
                nc.vector.tensor_tensor_reduce(score[:, cs], ps_s[c][:, :], adj_s[:, b, cs], 1.0, -3.0e38,
                                               ALU.add, ALU.max, chunk_max[:, c:c + 1]).then_inc(score_done, 1)

            def softmax_bias(t):
                dve.wait_ge(score_done, t * NG + NG)
                nc.vector.tensor_reduce(row_max[:, :], chunk_max[:, :], AX.X, ALU.max).then_inc(row_max_done, 1)
                dve.wait_ge(row_max_done, t + 1)
                nc.vector.scalar_tensor_tensor(out=top[:, :], in0=row_max[:, :], scalar=2.0,
                                               in1=c_row[:, bass.ds(t, 1)], op0=ALU.mult,
                                               op1=ALU.add).then_inc(top_done, 1)
                dve.wait_ge(top_done, t + 1)
                nc.vector.scalar_tensor_tensor(out=exp_bias[:, :], in0=c_row[:, bass.ds(t, 1)], scalar=P_SHIFT,
                                               in1=top[:, :], op0=ALU.add, op1=ALU.subtract).then_inc(bias_done, 1)

            def row_sum(t):
                dve.wait_ge(exp_done, t + 1)
                nc.vector.reciprocal(den_r[:, bass.ds(t, 1)], den[:, :]).then_inc(den_r_done, 1)

            def attend(t, b):
                dve.wait_ge(den_r_done, t + 1)
                if not isinstance(t, int) or t > 0:
                    dve.wait_ge(out_ready, t)
                else:
                    dve.wait_ge(x1_done, NT)
                residual(t + NT, xs[:, bass.ds(t, 1), :], b, den_r[:, bass.ds(t, 1)])

            def out_tile(t, b, reuse=True):
                if reuse:
                    dve.wait_ge(out_stored[b], dma_count(t - 2, b))
                normalise(t + NT, out_t[b][:, :], out_ready)

            def y_lo_tile(t, b):
                dve.wait_ge(y_hi_done, t + 1)
                nc.vector.tensor_tensor(yt_lo[b][:, :, :], y_t[:, :, bass.ts(t, P)], yt_hi[b][:, :, :],
                                        ALU.subtract).then_inc(y_lo_done, 1)

            def layer2_step(t, b, z=True, pv=True, y=True, reuse=True):
                if z:
                    attend(t - 2, b)
                if y:
                    y_lo_tile(t + 1, 1 - b)
                for c in range(NG):
                    score_chunk(t, b, c)
                    if c == 0 and pv:
                        row_sum(t - 1)
                    if pv:
                        lo_group((t + (NT - 1)) * NG + c, 1 - b, c, ps_t[c % 2])
                    if z and c == 1:
                        out_tile(t - 2, b, reuse)
                softmax_bias(t)

            y_lo_tile(0, 0)
            y_lo_tile(1, 1)
            xt_lo_tile(NT - 2)
            edge(NT - 1, 1)
            v_lo_tile(NT - 2)
            x1_tile(NT - 1, 1)
            score_chunk(0, 0, 0)
            score_chunk(0, 0, 1)
            xt_lo_tile(NT - 1)
            score_chunk(0, 0, 2)
            v_lo_tile(NT - 1)
            score_chunk(0, 0, 3)
            softmax_bias(0)
            dve.wait_ge(x1_kept, NT)
            layer2_step(1, 1, z=False)
            layer2_step(2, 0, reuse=False)
            layer2_step(3, 1, reuse=False)
            with dve.Fori(4, NT - 3, 2) as t:
                for b in range(2):
                    layer2_step(t + b, b)
            layer2_step(NT - 2, 0)
            layer2_step(NT - 1, 1, y=False)
            attend(NT - 2, 0)
            row_sum(NT - 1)
            for g in range(NG):
                lo_group((2 * NT - 1) * NG + g, 1, g, ps_t[g % 2])
                if g == 0:
                    out_tile(NT - 2, 0)
            attend(NT - 1, 1)
            out_tile(NT - 1, 1)


def kernel(x, adj, L1_gnn_Wq, L1_gnn_bq, L1_gnn_Wk, L1_gnn_bk, L1_gnn_Wv, L1_gnn_bv):
    import concourse.bacc as bacc
    from concourse.bass_utils import run_bass_kernel_spmd

    def blocks(b):
        return np.ascontiguousarray(np.asarray(b).reshape(-1, P).T)

    nc = bacc.Bacc("TRN2", target_bir_lowering=False, num_devices=1)
    arrays = {
        "x": np.ascontiguousarray(x),
        "adj": np.ascontiguousarray(adj),
        "wq": np.ascontiguousarray(L1_gnn_Wq),
        "wk": np.ascontiguousarray(L1_gnn_Wk),
        "wv_t": np.ascontiguousarray(np.asarray(L1_gnn_Wv).T),
        "bq": blocks(L1_gnn_bq),
        "bk": blocks(L1_gnn_bk),
        "bv": np.ascontiguousarray(np.broadcast_to(np.asarray(L1_gnn_bv), (P, L1_gnn_bv.shape[0]))),
    }
    args = [nc.dram_tensor(f"in_{k}", a.shape, mybir.dt.from_np(a.dtype), kind="ExternalInput").ap()
            for k, a in arrays.items()]
    out = nc.dram_tensor("out", arrays["x"].shape, F32, kind="ExternalOutput").ap()
    gnn_layers(nc, *args, out)
    result = run_bass_kernel_spmd(nc, [{f"in_{k}": a for k, a in arrays.items()}], core_ids=[0])
    return result.results[0]["out"]
```

```python
from contextlib import ExitStack

import numpy as np

import concourse.bass as bass
from concourse import mybir

F32 = mybir.dt.float32
F16 = mybir.dt.float16
BF16 = mybir.dt.bfloat16
ALU = mybir.AluOpType
ACT = mybir.ActivationFunctionType
AX = mybir.AxisListType

P = 128
LANES = 4
BANK = LANES * P

X_SCALE = 1.0 / 8
W_SCALE = 16.0
Y_SCALE = 1.0 / 4
P_SHIFT = 12 * float(np.log(2.0))
LN_EPS = 1e-5
HEAD_EPS = 1e-12


def gnn_layers(nc, x, adj, wq, wk, wv_t, bq, bk, bv, out):
    N, D = x.shape
    NT = N // P
    KD = D // P
    NG = N // BANK
    HALF = N // 2
    RING = 4
    QK_SCALE = 1.0 / (2.0 * float(np.sqrt(D)))
    assert N % BANK == 0 and KD == 2 and NT % RING == 0 and NT >= 10
    assert X_SCALE * Y_SCALE == QK_SCALE

    with ExitStack() as ctx:
        def sb(name, shape, dt=F32):
            return ctx.enter_context(nc.sbuf_tensor(name, shape, dt))

        def ps(name, shape, dt=F32):
            return ctx.enter_context(nc.psum_tensor(name, shape, dt))

        def sem(name):
            return ctx.enter_context(nc.semaphore(name))

        ident = sb("ident", [P, P])
        ones = sb("ones", [P, P])
        minus_half = sb("minus_half", [P, 1])
        xs = sb("xs", [P, NT, D])
        x_split = sb("x_split", [P, NT, 2 * D], F16)
        wq_s = sb("wq_s", [P, KD, D])
        wk_s = sb("wk_s", [P, KD, D])
        wv_s = sb("wv_s", [P, KD, D])
        bq_s = sb("bq_s", [P, KD])
        bk_s = sb("bk_s", [P, KD])
        bv_s = sb("bv_s", [P, D])
        bq_wide = sb("bq_wide", [P, KD, P])
        g_hi = sb("g_hi", [P, KD, D], F16)
        g_lo = sb("g_lo", [P, KD, D], F16)
        y_bias = sb("y_bias", [P, KD])
        wv_u = sb("wv_u", [P, KD, D + 2])
        wv_hi = sb("wv_hi", [P, KD, D + 2], F16)
        wv_lo = sb("wv_lo", [P, KD, D + 2], F16)
        c_bias = sb("c_bias", [P, 1])

        adj_s = sb("adj_s", [P, RING, N])
        score = adj_s[:, RING - 2, :]
        prob = adj_s[:, RING - 1, :]
        sign = sb("sign", [P, N], BF16)
        mask = sb("mask", [P, N], BF16)
        inc = [sb(f"inc{i}", [P, N]) for i in range(2)]
        count = sb("count", [P, 2])
        head_r = sb("head_r", [P, 2])
        t_hi = [sb(f"t_hi{i}", [P, NT, P], F16) for i in range(2)]
        t_lo = [sb(f"t_lo{i}", [P, NT, P], F16) for i in range(2)]
        deg = sb("deg", [P, 1])
        count_parts = sb("count_parts", [P, 2, 2])
        deg_parts = sb("deg_parts", [P, 2, NG])
        deg_r = sb("deg_r", [P, NT])
        z = sb("z", [P, D])
        stats = sb("stats", [P, 6])
        mv = sb("mv", [P, 2])
        var_eps = sb("var_eps", [P, 1])
        rstd = sb("rstd", [P, 1])
        x1_t = [sb(f"x1_t{i}", [P, D]) for i in range(2)]
        xt_hi = sb("xt_hi", [P, KD, N], F16)
        xt_lo = sb("xt_lo", [P, KD, N], F16)
        v_split = sb("v_split", [P, NT, 2 * D], F16)
        c_row = sb("c_row", [P, NT])
        y_t = sb("y_t", [P, KD, N])
        yt_hi = [sb(f"yt_hi{i}", [P, KD, P], F16) for i in range(2)]
        yt_lo = [sb(f"yt_lo{i}", [P, KD, P], F16) for i in range(2)]
        chunk_max = sb("chunk_max", [P, NG])
        row_max = sb("row_max", [P, 1])
        top = sb("top", [P, 1])
        exp_bias = sb("exp_bias", [P, 1])
        den = sb("den", [P, 1])
        den_r = sb("den_r", [P, NT])
        out_t = [sb(f"out_t{i}", [P, D]) for i in range(2)]

        ps_o = [ps(f"ps_o{i}", [P, BANK]) for i in range(2)]
        ps_s = [ps(f"ps_s{i}", [P, BANK]) for i in range(NG)]
        ps_t = [ps(f"ps_t{i}", [P, BANK]) for i in range(2)]
        ps_xt, ps_v = ps_t
        ps_y = ps_xt
        ps_w, ps_b = ps_t

        adj_loaded = [sem(f"adj_loaded{i}") for i in range(2)]
        adj_half_loaded = [sem(f"adj_half_loaded{i}") for i in range(2)]
        x_loaded = [sem(f"x_loaded{i}") for i in range(NG)]
        w_loaded = sem("w_loaded")
        wv_loaded = sem("wv_loaded")
        const_ready = sem("const_ready")
        ident_ready = sem("ident_ready")
        x_hi_done = sem("x_hi_done")
        x_lo_done = sem("x_lo_done")
        bq_wide_done = sem("bq_wide_done")
        g_done = sem("g_done")
        g_hi_done = sem("g_hi_done")
        g_split_done = sem("g_split_done")
        w_bias_done = sem("w_bias_done")
        wv_u_done = sem("wv_u_done")
        wv_hi_done = sem("wv_hi_done")
        sign_done = sem("sign_done")
        mask_part_done = sem("mask_part_done")
        count_done = sem("count_done")
        head_floor = sem("head_floor")
        head_done = sem("head_done")
        inc_part_done = sem("inc_part_done")
        inc_done = sem("inc_done")
        trans_done = sem("trans_done")
        hi_done = sem("hi_done")
        lo_done = sem("lo_done")
        prod_done = sem("prod_done")
        deg_r_done = sem("deg_r_done")
        z_done = sem("z_done")
        stats_done = sem("stats_done")
        mv_done = sem("mv_done")
        var_done = sem("var_done")
        rstd_done = sem("rstd_done")
        x1_done = sem("x1_done")
        x1_kept = sem("x1_kept")
        xt_done = sem("xt_done")
        xt_hi_done = sem("xt_hi_done")
        xt_lo_done = sem("xt_lo_done")
        v_done = sem("v_done")
        v_hi_done = sem("v_hi_done")
        v_lo_done = sem("v_lo_done")
        y_done = sem("y_done")
        y_kept = sem("y_kept")
        y_hi_done = sem("y_hi_done")
        y_lo_done = sem("y_lo_done")
        qk_done = sem("qk_done")
        score_done = sem("score_done")
        row_max_done = sem("row_max_done")
        top_done = sem("top_done")
        bias_done = sem("bias_done")
        exp_done = sem("exp_done")
        den_r_done = sem("den_r_done")
        out_ready = sem("out_ready")
        out_stored = [sem(f"out_stored{i}") for i in range(2)]

        adj_rows = adj.rearrange("(t p) n -> t p n", p=P)
        out_rows = out.rearrange("(t p) d -> t p d", p=P)
        x_rows = x.rearrange("(t p) d -> p t d", p=P)
        XT = NT // NG

        def dma_count(n, b):
            return (n + 2 - b) * 8

        def wait_apart(eng, settled, *awaited):
            for reg, _, value in awaited:
                eng.reg_mov(reg, value)
            eng.wait_ge(settled, 1)
            for reg, semaphore, _ in awaited:
                eng.wait_ge(semaphore, reg)

        block = ctx.enter_context(nc.Block())

        @block.sync
        def _(sp):
            def load_adj1(n, slot):
                if not isinstance(n, int) or n >= RING:
                    sp.wait_ge(count_done, n - 1)
                sp.dma_start(adj_s[:, slot, :], adj_rows[n, :, :]).then_inc(adj_loaded[slot % 2], 16)

            def load_adj2(t, b, first=False):
                if first:
                    sp.wait_ge(count_done, NT + t - 1)
                else:
                    sp.wait_ge(score_done, (t - 1) * NG)
                sp.dma_start(adj_s[:, b, :], adj_rows[t, :, :]).then_inc(adj_loaded[b], 16)

            def store_out(t, b):
                sp.wait_ge(out_ready, t + 1)
                sp.dma_start(out_rows[t, :, :], out_t[b][:, :]).then_inc(out_stored[b], 16)

            def load_halves(n):
                sp.dma_start(adj_s[:, n, 0:HALF], adj_rows[n, :, 0:HALF]).then_inc(adj_half_loaded[n], 16)
                sp.dma_start(adj_s[:, n, HALF:N], adj_rows[n, :, HALF:N]).then_inc(adj_loaded[n], 16)

            def load_x(g):
                ts = slice(g * XT, (g + 1) * XT)
                sp.dma_start(xs[:, ts, :], x_rows[:, ts, :]).then_inc(x_loaded[g], 16)

            load_halves(0)
            sp.dma_start(bq_s[:, :], bq).then_inc(w_loaded, 16)
            for name, src in ((wq_s, wq), (wk_s, wk)):
                sp.dma_start(name[:, :, :], src.rearrange("(k p) d -> p k d", p=P)).then_inc(w_loaded, 16)
            sp.dma_start(bk_s[:, :], bk).then_inc(w_loaded, 16)
            load_x(0)
            load_x(1)
            load_halves(1)
            load_x(2)
            load_x(3)
            sp.wait_ge(adj_loaded[0], 16)
            load_adj1(2, 2)
            sp.dma_start(wv_s[:, :, :], wv_t.rearrange("(k p) d -> p k d", p=P)).then_inc(wv_loaded, 16)
            sp.dma_start(bv_s[:, :], bv).then_inc(wv_loaded, 16)
            sp.wait_ge(adj_loaded[1], 16)
            load_adj1(3, 3)
            with sp.Fori(RING, NT - RING + 1, RING) as n:
                for slot in range(RING):
                    load_adj1(n + slot, slot)
            for b in range(2):
                load_adj2(b, b, first=True)
            load_adj2(2, 0)
            load_adj2(3, 1)
            with sp.Fori(2, NT - 3, 2) as t:
                for b in range(2):
                    load_adj2(t + b + 2, b)
                    store_out(t + b - 2, b)
            for t in range(NT - 4, NT):
                store_out(t, t % 2)
            for b in range(2):
                sp.wait_ge(out_stored[b], 16 * (NT // 2))

        @block.gpsimd
        def _(pool):
            pool_value = pool.alloc_register("pool_value")
            nc.gpsimd.memset(minus_half[:, :], -0.5).then_inc(const_ready, 1)
            nc.gpsimd.memset(ones[:, :], 1.0).then_inc(const_ready, 1)
            nc.gpsimd.memset(ident[:, :], 0.0).then_inc(const_ready, 1)
            pool.wait_ge(const_ready, 3)
            nc.gpsimd.affine_select(out=ident[:, :], in_=ident[:, :], compare_op=ALU.not_equal, fill=1.0,
                                    base=0, pattern=[[-1, P]], channel_multiplier=1).then_inc(ident_ready, 1)

            def head_norm(n, b):
                wait_apart(pool, const_ready, (pool_value, count_done, n + 1))
                nc.gpsimd.tensor_scalar(head_r[:, b:b + 1], count[:, b:b + 1], HEAD_EPS ** 2, None,
                                        ALU.max).then_inc(head_floor, 1)
                pool.wait_ge(head_floor, n + 1)
                nc.gpsimd.tensor_tensor(head_r[:, b:b + 1], head_r[:, b:b + 1], minus_half[:, :],
                                        ALU.pow).then_inc(head_done, 1)

            def row_rstd(n):
                pool.wait_ge(var_done, n + 1)
                nc.gpsimd.tensor_tensor(rstd[:, :], var_eps[:, :], minus_half[:, :],
                                        ALU.pow).then_inc(rstd_done, 1)

            def keep_x1(t, b):
                pool.wait_ge(x1_done, t + 1)
                nc.gpsimd.tensor_tensor(xs[:, bass.ds(t, 1), :], x1_t[b][:, :], bv_s[:, :],
                                        ALU.add).then_inc(x1_kept, 1)

            def x_lo_part(g):
                ts = slice(g * XT, (g + 1) * XT)
                pool.wait_ge(x_hi_done, g + 1)
                nc.gpsimd.tensor_tensor(x_split[:, ts, D:2 * D], xs[:, ts, :], x_split[:, ts, 0:D],
                                        ALU.subtract).then_inc(x_lo_done, 1)

            head_norm(0, 0)
            x_lo_part(0)
            x_lo_part(1)
            head_norm(1, 1)
            x_lo_part(2)
            x_lo_part(3)
            pool.wait_ge(wv_loaded, 16 * 2)
            nc.gpsimd.tensor_scalar(wv_u[:, :, 0:D], wv_s[:, :, :], W_SCALE, None, ALU.mult).then_inc(wv_u_done, 1)
            head_norm(2, 0)
            row_rstd(0)
            keep_x1(0, 0)
            head_norm(3, 1)
            pool.wait_ge(wv_hi_done, 1)
            nc.gpsimd.tensor_tensor(wv_lo[:, :, :], wv_u[:, :, :], wv_hi[:, :, :],
                                    ALU.subtract).then_inc(wv_hi_done, 1)
            row_rstd(1)
            head_norm(4, 0)
            keep_x1(1, 1)
            with pool.Fori(2, NT - 5, 2) as t:
                for b in range(2):
                    head_norm(t + b + 3, 1 - b)
                    row_rstd(t + b)
                    keep_x1(t + b, b)
            head_norm(NT - 1, 1)
            for t in range(NT - 4, NT):
                row_rstd(t)
                keep_x1(t, t % 2)
            with pool.Fori(0, NT) as t:
                row_rstd(t + NT)

        @block.tensor
        def _(pe):
            def weight_product():
                pe.wait_ge(w_loaded, 16 * 4)
                for m in range(KD):
                    for k in range(KD):
                        nc.tensor.matmul(ps_w[:, m * D:(m + 1) * D], wq_s[:, k, m * P:(m + 1) * P],
                                         wk_s[:, k, :], start=(k == 0), stop=(k == KD - 1))

            def weight_biases():
                for m in range(KD):
                    for k in range(KD):
                        nc.tensor.matmul(ps_b[:, m:m + 1], wk_s[:, k, m * P:(m + 1) * P], bq_s[:, k:k + 1],
                                         start=(k == 0), stop=(k == KD - 1))
                for m in range(KD):
                    for k in range(KD):
                        nc.tensor.matmul(ps_b[:, KD + m:KD + m + 1], wq_s[:, k, m * P:(m + 1) * P],
                                         bk_s[:, k:k + 1], start=(k == 0), stop=(k == KD - 1))
                pe.wait_ge(bq_wide_done, KD)
                for k in range(KD):
                    last = nc.tensor.matmul(ps_b[:, 2 * KD:2 * KD + 1], bq_wide[:, k, :], bk_s[:, k:k + 1],
                                            start=(k == 0), stop=(k == KD - 1))
                last.then_inc(g_done, 1)

            def transpose_group(src, g, bank):
                for i in range(LANES):
                    c = (g * LANES + i) * P
                    last = nc.tensor.transpose(bank[:, i * P:(i + 1) * P], src[:, c:c + P], ident[:, :])
                last.then_inc(trans_done, 1)

            def product_group(b, g, right):
                for j in range(g * LANES, (g + 1) * LANES):
                    for a, (left, c) in enumerate(((t_hi[b], 0), (t_hi[b], D), (t_lo[b], 0))):
                        last = nc.tensor.matmul(ps_o[b][:, 0:D], left[:, j, :], right[:, j, c:c + D],
                                                start=(j == 0 and a == 0), stop=(j == NT - 1 and a == 2))
                if g == NG - 1:
                    last.then_inc(prod_done, 1)

            def x1_transpose(t, b, first=False):
                pe.wait_ge(x1_done, t + 1)
                if first:
                    pe.wait_ge(g_split_done, KD)
                else:
                    pe.wait_ge(y_kept, t * KD)
                for k in range(KD):
                    last = nc.tensor.transpose(ps_xt[:, k * P:(k + 1) * P], x1_t[b][:, k * P:(k + 1) * P],
                                               ident[:, :])
                last.then_inc(xt_done, 1)

            def v_y_product(t, first=False):
                pe.wait_ge(xt_lo_done, t + 1)
                if first:
                    pe.wait_ge(wv_hi_done, 2)
                else:
                    pe.wait_ge(v_lo_done, t)
                xh = [xt_hi[:, k, bass.ts(t, P)] for k in range(KD)]
                xl = [xt_lo[:, k, bass.ts(t, P)] for k in range(KD)]
                for k in range(KD):
                    for a, (left, right) in enumerate(((xh, wv_hi), (xh, wv_lo), (xl, wv_hi))):
                        last = nc.tensor.matmul(ps_v[:, 0:D + 2], left[k], right[:, k, :],
                                                start=(k == 0 and a == 0), stop=(k == KD - 1 and a == 2))
                last.then_inc(v_done, 1)
                for m in range(KD):
                    gs = slice(m * P, (m + 1) * P)
                    for k in range(KD):
                        for a, (left, right) in enumerate(((g_hi, xh), (g_hi, xl), (g_lo, xh))):
                            last = nc.tensor.matmul(ps_y[:, gs], left[:, k, gs], right[k],
                                                    start=(k == 0 and a == 0), stop=(k == KD - 1 and a == 2))
                last.then_inc(y_done, 1)

            def layer1_step(t, b, trans=((0,), (1,), (2,), (3,)), prod=True, vy=1, early_xt=True, late_xt=None):
                for g in range(NG):
                    pe.wait_ge(lo_done, t * NG + (g + 1 - NG))
                    if prod:
                        if g == 0:
                            pe.wait_ge(z_done, t - 2)
                        product_group(1 - b, g, x_split)
                        if g == 0 and late_xt:
                            x1_transpose(t - 3, 1 - b, first=(late_xt == "first"))
                        if g == vy:
                            v_y_product(t - 3, first=(late_xt == "first"))
                    if trans:
                        for i in trans[g]:
                            if i == 0:
                                pe.wait_ge(inc_done, t + 1)
                            transpose_group(inc[b], i, ps_s[i])
                    elif g == NG - 2:
                        x1_transpose(t - 2, b)
                if trans and early_xt:
                    x1_transpose(t - 2, b)

            pe.wait_ge(ident_ready, 1)
            weight_product()
            for g in range(NG):
                pe.wait_ge(inc_part_done, g + 1)
                transpose_group(inc[0], g, ps_s[g])
            for g in range(NG):
                pe.wait_ge(x_hi_done, g + 1)
                pe.wait_ge(lo_done, g + 1)
                for j in range(g * LANES, (g + 1) * LANES):
                    for left in (t_hi[0], t_lo[0]):
                        nc.tensor.matmul(ps_o[0][:, 0:D], left[:, j, :], x_split[:, j, 0:D],
                                         start=(j == 0 and left is t_hi[0]), stop=False)
                if g == 1:
                    weight_biases()
            for g in range(NG):
                pe.wait_ge(x_lo_done, g + 1)
                for j in range(g * LANES, (g + 1) * LANES):
                    last = nc.tensor.matmul(ps_o[0][:, 0:D], t_hi[0][:, j, :], x_split[:, j, D:2 * D],
                                            start=False, stop=(j == NT - 1))
                if g == 1:
                    for i in range(NG):
                        pe.wait_ge(inc_part_done, NG + i + 1)
                        transpose_group(inc[1], i, ps_s[i])
            last.then_inc(prod_done, 1)
            for g in range(NG):
                pe.wait_ge(lo_done, NG + g + 1)
                product_group(1, g, x_split)
            layer1_step(2, 0, prod=False, early_xt=False)
            layer1_step(3, 1, trans=((), (), (0, 1), (2, 3)), vy=2, early_xt=False, late_xt="first")
            layer1_step(4, 0, trans=((), (0, 1), (2,), (3,)), vy=2, late_xt="second")
            layer1_step(5, 1)
            with pe.Fori(6, NT - 1, 2) as t:
                for b in range(2):
                    layer1_step(t + b, b)
            layer1_step(NT, 0, trans=None)

            def qk_chunk(t, b, c, first=False):
                if c == 0:
                    pe.wait_ge(y_lo_done, t + 1)
                if not first:
                    pe.wait_ge(score_done, t * NG + (c + 1 - NG))
                cs = slice(c * BANK, (c + 1) * BANK)
                for k in range(KD):
                    for a, (left, right) in enumerate(((yt_hi[b], xt_hi), (yt_hi[b], xt_lo), (yt_lo[b], xt_hi))):
                        last = nc.tensor.matmul(ps_s[c][:, :], left[:, k, :], right[:, k, cs],
                                                start=(k == 0 and a == 0), stop=(k == KD - 1 and a == 2))
                last.then_inc(qk_done, 1)

            def prob_transposes(t, c, reuse=True):
                if c == 0:
                    pe.wait_ge(exp_done, t + 1)
                if reuse:
                    pe.wait_ge(lo_done, (t + NT) * NG + (c - 1))
                transpose_group(prob, c, ps_t[c % 2])

            def prob_product(t, b, g):
                if g == 0:
                    pe.wait_ge(z_done, t + (NT - 1))
                pe.wait_ge(lo_done, (t + NT) * NG + g + 1)
                product_group(b, g, v_split)

            def layer2_step(t, b):
                for c in range(NG):
                    qk_chunk(t, b, c)
                    prob_transposes(t - 1, c)
                for g in range(NG):
                    prob_product(t - 1, 1 - b, g)

            v_y_product(NT - 2)
            pe.wait_ge(lo_done, NT * NG)
            qk_chunk(0, 0, 0, first=True)
            x1_transpose(NT - 1, 1)
            for c in range(1, NG):
                if c == NG - 1:
                    pe.wait_ge(xt_lo_done, NT)
                qk_chunk(0, 0, c, first=True)
            v_y_product(NT - 1)
            qk_chunk(1, 1, 0)
            qk_chunk(1, 1, 1)
            pe.wait_ge(y_kept, NT * KD)
            pe.wait_ge(v_lo_done, NT)
            for c in range(NG):
                prob_transposes(0, c, reuse=(c >= 2))
                if c < NG - 2:
                    qk_chunk(1, 1, c + 2)
            for g in range(NG):
                prob_product(0, 0, g)
            with pe.Fori(2, NT - 3, 2) as t:
                for b in range(2):
                    layer2_step(t + b, b)
            layer2_step(NT - 2, 0)
            for c in range(NG):
                qk_chunk(NT - 1, 1, c)
                prob_transposes(NT - 2, c)
            for g in range(NG):
                prob_product(NT - 2, 0, g)
                if g == NG - 2:
                    pe.wait_ge(exp_done, NT)
                    for c in range(NG):
                        transpose_group(prob, c, ps_s[c])
            for g in range(NG):
                prob_product(NT - 1, 1, g)

        @block.scalar
        def _(act):
            def sign_tile(n, b):
                act.wait_ge(adj_loaded[b], dma_count(n, b))
                if not isinstance(n, int) or n > 2:
                    act.wait_ge(count_done, n)
                nc.scalar.activation(sign[:, :], adj_s[:, bass.ds(n % RING, 1), :], ACT.Sign).then_inc(sign_done, 1)

            def mask_tile(n, b):
                act.wait_ge(inc_done, n)
                act.wait_ge(sign_done, n - 1)
                nc.scalar.activation(mask[:, :], sign[:, :], ACT.Relu,
                                     accum_out=count[:, b:b + 1]).then_inc(count_done, 1)

            def hi_group(n, b, g, bank):
                act.wait_ge(trans_done, n + 1)
                nc.scalar.copy(t_hi[b][:, g * LANES:(g + 1) * LANES, :], bank[:, :]).then_inc(hi_done, 1)

            def xt_hi_tile(t):
                act.wait_ge(xt_done, t + 1)
                nc.scalar.activation(xt_hi[:, :, bass.ts(t, P)],
                                     ps_xt[:, 0:KD * P].rearrange("p (k n) -> p k n", k=KD),
                                     ACT.Copy, scale=X_SCALE).then_inc(xt_hi_done, 1)

            def v_y_tile(t):
                act.wait_ge(v_done, t + 1)
                nc.scalar.activation(c_row[:, bass.ds(t, 1)], ps_v[:, D:D + 1], ACT.Identity,
                                     scale=2 * QK_SCALE / (X_SCALE * W_SCALE), bias=c_bias[:, :])
                nc.scalar.activation(v_split[:, bass.ds(t, 1), 0:D], ps_v[:, 0:D], ACT.Copy,
                                     scale=1.0 / (X_SCALE * W_SCALE)).then_inc(v_hi_done, 1)
                act.wait_ge(y_done, t + 1)
                for m in range(KD):
                    nc.scalar.activation(y_t[:, m, bass.ts(t, P)], ps_y[:, m * P:(m + 1) * P], ACT.Identity,
                                         scale=Y_SCALE / (X_SCALE * W_SCALE),
                                         bias=y_bias[:, m:m + 1]).then_inc(y_kept, 1)

            def x_hi_part(g):
                ts = slice(g * XT, (g + 1) * XT)
                act.wait_ge(x_loaded[g], 16)
                nc.scalar.copy(x_split[:, ts, 0:D], xs[:, ts, :]).then_inc(x_hi_done, 1)

            def layer1_step(t, b, trans=True, ahead=True):
                xt_hi_tile(t - 3)
                if trans:
                    act.wait_ge(prod_done, t - 1)
                for g in range(NG):
                    if trans:
                        hi_group(t * NG + g, b, g, ps_s[g])
                    if g == 0:
                        v_y_tile(t - 3)
                    if g == 1 and ahead:
                        sign_tile(t + 2, b)
                    if g == 2 and ahead:
                        mask_tile(t + 2, b)

            x_hi_part(0)
            x_hi_part(1)
            for g in range(NG):
                hi_group(g, 0, g, ps_s[g])
            x_hi_part(2)
            x_hi_part(3)
            act.wait_ge(g_done, 1)
            for m in range(KD):
                nc.scalar.activation(g_hi[:, m, :], ps_w[:, m * D:(m + 1) * D], ACT.Copy,
                                     scale=W_SCALE).then_inc(g_hi_done, 1)
            sign_tile(2, 0)
            hi_group(NG, 1, 0, ps_s[0])
            hi_group(NG + 1, 1, 1, ps_s[1])
            mask_tile(2, 0)
            hi_group(NG + 2, 1, 2, ps_s[2])
            hi_group(NG + 3, 1, 3, ps_s[3])
            sign_tile(3, 1)
            act.wait_ge(prod_done, 1)
            hi_group(2 * NG, 0, 0, ps_s[0])
            hi_group(2 * NG + 1, 0, 1, ps_s[1])
            mask_tile(3, 1)
            hi_group(2 * NG + 2, 0, 2, ps_s[2])
            xt_hi_tile(0)
            act.wait_ge(wv_u_done, 1 + KD)
            nc.scalar.copy(wv_hi[:, :, :], wv_u[:, :, :]).then_inc(wv_hi_done, 1)
            act.wait_ge(w_bias_done, 2)
            hi_group(2 * NG + 3, 0, 3, ps_s[3])
            sign_tile(4, 0)
            mask_tile(4, 0)
            act.wait_ge(prod_done, 2)
            hi_group(3 * NG, 1, 0, ps_s[0])
            hi_group(3 * NG + 1, 1, 1, ps_s[1])
            v_y_tile(0)
            hi_group(3 * NG + 2, 1, 2, ps_s[2])
            hi_group(3 * NG + 3, 1, 3, ps_s[3])
            xt_hi_tile(1)
            sign_tile(5, 1)
            mask_tile(5, 1)
            act.wait_ge(prod_done, 3)
            hi_group(4 * NG, 0, 0, ps_s[0])
            hi_group(4 * NG + 1, 0, 1, ps_s[1])
            sign_tile(6, 0)
            v_y_tile(1)
            hi_group(4 * NG + 2, 0, 2, ps_s[2])
            mask_tile(6, 0)
            hi_group(4 * NG + 3, 0, 3, ps_s[3])
            layer1_step(5, 1)
            with act.Fori(6, NT - 3, 2) as t:
                for b in range(2):
                    layer1_step(t + b, b)
            layer1_step(NT - 2, 0, ahead=False)
            layer1_step(NT - 1, 1, ahead=False)
            layer1_step(NT, 0, trans=False, ahead=False)

            def y_hi_tile(t, b):
                nc.scalar.copy(yt_hi[b][:, :, :], y_t[:, :, bass.ts(t, P)]).then_inc(y_hi_done, 1)

            def layer2_step(t, b, pv=True, y=True):
                if y:
                    act.wait_ge(qk_done, t * NG)
                    y_hi_tile(t + 1, 1 - b)
                if pv:
                    for g in range(NG):
                        hi_group((t + (NT - 1)) * NG + g, 1 - b, g, ps_t[g % 2])
                    act.wait_ge(den_r_done, t)
                act.wait_ge(bias_done, t + 1)
                nc.scalar.activation(prob, score, ACT.Exp, scale=2.0, bias=exp_bias[:, :],
                                     accum_out=den[:, :]).then_inc(exp_done, 1)

            act.wait_ge(y_kept, 2 * KD)
            y_hi_tile(0, 0)
            y_hi_tile(1, 1)
            xt_hi_tile(NT - 2)
            v_y_tile(NT - 2)
            xt_hi_tile(NT - 1)
            v_y_tile(NT - 1)
            act.wait_ge(y_kept, NT * KD)
            layer2_step(0, 0, pv=False, y=False)
            with act.Fori(1, NT - 2, 2) as t:
                for b in range(2):
                    layer2_step(t + b, 1 - b)
            layer2_step(NT - 1, 1, y=False)
            for g in range(NG):
                hi_group((2 * NT - 1) * NG + g, 1, g, ps_s[g])

        @block.vector
        def _(dve):
            dve_value = dve.alloc_register("dve_value")

            def inc_tile(n, b):
                dve.wait_ge(head_done, n + 1)
                if not isinstance(n, int) or n >= 2:
                    dve.wait_ge(trans_done, (n - 1) * NG)
                dve.wait_ge(deg_r_done, n)
                nc.vector.scalar_tensor_tensor(
                    out=inc[b][:, :], in0=mask[:, :], scalar=head_r[:, b:b + 1],
                    in1=adj_s[:, bass.ds(n % RING, 1), :],
                    op0=ALU.mult, op1=ALU.add, accum_out=deg[:, :]).then_inc(inc_done, 1)
                dve.wait_ge(inc_done, n + 1)
                nc.vector.reciprocal(deg_r[:, bass.ds(n, 1)], deg[:, :]).then_inc(deg_r_done, 1)

            def lo_group(n, b, g, bank):
                dve.wait_ge(hi_done, n + 1)
                nc.vector.tensor_tensor(t_lo[b][:, g * LANES:(g + 1) * LANES, :],
                                        bank[:, :].rearrange("p (a n) -> p a n", a=LANES),
                                        t_hi[b][:, g * LANES:(g + 1) * LANES, :],
                                        ALU.subtract).then_inc(lo_done, 1)

            def residual(n, base, b, scale):
                dve.wait_ge(prod_done, n + 1)
                nc.vector.scalar_tensor_tensor(out=z[:, :], in0=ps_o[b][:, 0:D], scalar=scale,
                                               in1=base, op0=ALU.mult, op1=ALU.add).then_inc(z_done, 1)
                dve.wait_ge(z_done, n + 1)
                nc.vector.bn_stats(stats[:, :], z[:, :]).then_inc(stats_done, 1)
                wait_apart(dve, const_ready, (dve_value, stats_done, n + 1))
                nc.vector.bn_aggr(mv[:, :], stats[:, :]).then_inc(mv_done, 1)
                dve.wait_ge(mv_done, n + 1)
                nc.vector.tensor_scalar(var_eps[:, :], mv[:, 1:2], LN_EPS, None, ALU.add).then_inc(var_done, 1)

            def normalise(n, dst, done):
                dve.wait_ge(rstd_done, n + 1)
                nc.vector.tensor_scalar(dst, z[:, :], mv[:, 0:1], rstd[:, :], ALU.subtract,
                                        ALU.mult).then_inc(done, 1)

            def edge(t, b):
                dve.wait_ge(deg_r_done, t + 1)
                if not isinstance(t, int) or t > 0:
                    dve.wait_ge(x1_done, t)
                residual(t, xs[:, bass.ds(t, 1), :], b, deg_r[:, bass.ds(t, 1)])

            def x1_tile(t, b, reuse=True):
                if reuse:
                    dve.wait_ge(xt_done, t - 1)
                    dve.wait_ge(x1_kept, t - 1)
                normalise(t, x1_t[b][:, :], x1_done)

            def xt_lo_tile(t):
                dve.wait_ge(xt_hi_done, t + 1)
                nc.vector.scalar_tensor_tensor(out=xt_lo[:, :, bass.ts(t, P)],
                                               in0=ps_xt[:, 0:KD * P].rearrange("p (k n) -> p k n", k=KD),
                                               scalar=X_SCALE, in1=xt_hi[:, :, bass.ts(t, P)],
                                               op0=ALU.mult, op1=ALU.subtract).then_inc(xt_lo_done, 1)

            def v_lo_tile(t):
                dve.wait_ge(v_hi_done, t + 1)
                nc.vector.scalar_tensor_tensor(out=v_split[:, bass.ds(t, 1), D:2 * D], in0=ps_v[:, 0:D],
                                               scalar=1.0 / (X_SCALE * W_SCALE),
                                               in1=v_split[:, bass.ds(t, 1), 0:D],
                                               op0=ALU.mult, op1=ALU.subtract).then_inc(v_lo_done, 1)

            def layer1_step(t, b, trans=True, ahead=True):
                xt_lo_tile(t - 3)
                edge(t - 2, b)
                if trans:
                    lo_group(t * NG, b, 0, ps_s[0])
                if ahead:
                    inc_tile(t + 1, 1 - b)
                x1_tile(t - 2, b)
                if trans:
                    lo_group(t * NG + 1, b, 1, ps_s[1])
                v_lo_tile(t - 3)
                if trans:
                    lo_group(t * NG + 2, b, 2, ps_s[2])
                    lo_group(t * NG + 3, b, 3, ps_s[3])

            def first_mask(n, h):
                hs = slice(h * HALF, (h + 1) * HALF)
                dve.wait_ge((adj_half_loaded, adj_loaded)[h][n], 16)
                nc.vector.tensor_scalar(mask[:, hs], adj_s[:, n, hs], 0.0, 0.0, ALU.is_gt, ALU.add,
                                        accum_out=count_parts[:, n, h:h + 1]).then_inc(mask_part_done, 1)

            def first_count(n):
                dve.wait_ge(mask_part_done, 2 * n + 2)
                nc.vector.tensor_tensor(count[:, n:n + 1], count_parts[:, n, 0:1], count_parts[:, n, 1:2],
                                        ALU.add).then_inc(count_done, 1)

            def first_inc(n, g):
                gs = slice(g * BANK, (g + 1) * BANK)
                nc.vector.scalar_tensor_tensor(
                    out=inc[n][:, gs], in0=mask[:, gs], scalar=head_r[:, n:n + 1], in1=adj_s[:, n, gs],
                    op0=ALU.mult, op1=ALU.add, accum_out=deg_parts[:, n, g:g + 1]).then_inc(inc_part_done, 1)

            def first_degree(n):
                dve.wait_ge(inc_part_done, (n + 1) * NG)
                nc.vector.tensor_reduce(deg[:, :], deg_parts[:, n, :], AX.X, ALU.add).then_inc(inc_done, 1)
                dve.wait_ge(inc_done, n + 1)
                nc.vector.reciprocal(deg_r[:, n:n + 1], deg[:, :]).then_inc(deg_r_done, 1)

            first_mask(0, 0)
            first_mask(0, 1)
            first_count(0)
            dve.wait_ge(w_loaded, 16 * 4)
            dve.wait_ge(const_ready, 2)
            for k in range(KD):
                nc.vector.tensor_scalar(bq_wide[:, k, :], ones[:, :], bq_s[:, k:k + 1], None,
                                        ALU.mult).then_inc(bq_wide_done, 1)
            dve.wait_ge(head_done, 1)
            for g in range(NG):
                first_inc(0, g)
            first_degree(0)
            for g in range(NG - 1):
                lo_group(g, 0, g, ps_s[g])
            first_mask(1, 0)
            first_mask(1, 1)
            first_count(1)
            lo_group(3, 0, 3, ps_s[3])
            dve.wait_ge(head_done, 2)
            for g in range(NG):
                first_inc(1, g)
            dve.wait_ge(deg_r_done, 1)
            first_degree(1)
            lo_group(NG, 1, 0, ps_s[0])
            lo_group(NG + 1, 1, 1, ps_s[1])
            edge(0, 0)
            lo_group(NG + 2, 1, 2, ps_s[2])
            lo_group(NG + 3, 1, 3, ps_s[3])
            inc_tile(2, 0)
            dve.wait_ge(g_done, 1)
            nc.vector.tensor_scalar(y_bias[:, :], ps_b[:, 0:KD], Y_SCALE, None, ALU.mult).then_inc(w_bias_done, 1)
            nc.vector.tensor_scalar(c_bias[:, :], ps_b[:, 2 * KD:2 * KD + 1], 2 * QK_SCALE, None,
                                    ALU.mult).then_inc(w_bias_done, 1)
            for k in range(KD):
                nc.vector.tensor_scalar(wv_u[:, k, D:D + 2], ps_b[:, KD + k:KD + k + 1].to_broadcast([P, 2]),
                                        W_SCALE, None, ALU.mult).then_inc(wv_u_done, 1)
            x1_tile(0, 0, reuse=False)
            lo_group(2 * NG, 0, 0, ps_s[0])
            dve.wait_ge(g_hi_done, KD)
            for m in range(KD):
                nc.vector.scalar_tensor_tensor(out=g_lo[:, m, :], in0=ps_w[:, m * D:(m + 1) * D], scalar=W_SCALE,
                                               in1=g_hi[:, m, :], op0=ALU.mult,
                                               op1=ALU.subtract).then_inc(g_split_done, 1)
            lo_group(2 * NG + 1, 0, 1, ps_s[1])
            lo_group(2 * NG + 2, 0, 2, ps_s[2])
            xt_lo_tile(0)
            inc_tile(3, 1)
            lo_group(2 * NG + 3, 0, 3, ps_s[3])
            edge(1, 1)
            lo_group(3 * NG, 1, 0, ps_s[0])
            x1_tile(1, 1, reuse=False)
            lo_group(3 * NG + 1, 1, 1, ps_s[1])
            inc_tile(4, 0)
            v_lo_tile(0)
            lo_group(3 * NG + 2, 1, 2, ps_s[2])
            lo_group(3 * NG + 3, 1, 3, ps_s[3])
            xt_lo_tile(1)
            edge(2, 0)
            lo_group(4 * NG, 0, 0, ps_s[0])
            x1_tile(2, 0)
            inc_tile(5, 1)
            lo_group(4 * NG + 1, 0, 1, ps_s[1])
            lo_group(4 * NG + 2, 0, 2, ps_s[2])
            v_lo_tile(1)
            lo_group(4 * NG + 3, 0, 3, ps_s[3])
            layer1_step(5, 1)
            with dve.Fori(6, NT - 3, 2) as t:
                for b in range(2):
                    layer1_step(t + b, b)
            layer1_step(NT - 2, 0)
            layer1_step(NT - 1, 1, ahead=False)
            layer1_step(NT, 0, trans=False, ahead=False)

            def score_chunk(t, b, c):
                if c == 0:
                    dve.wait_ge(adj_loaded[b], dma_count(t + NT, b))
                    if not isinstance(t, int) or t > 0:
                        dve.wait_ge(exp_done, t)
                wait_apart(dve, const_ready, (dve_value, qk_done, t * NG + c + 1))
                cs = slice(c * BANK, (c + 1) * BANK)
                nc.vector.tensor_tensor_reduce(score[:, cs], ps_s[c][:, :], adj_s[:, b, cs], 1.0, -3.0e38,
                                               ALU.add, ALU.max, chunk_max[:, c:c + 1]).then_inc(score_done, 1)

            def softmax_bias(t):
                dve.wait_ge(score_done, t * NG + NG)
                nc.vector.tensor_reduce(row_max[:, :], chunk_max[:, :], AX.X, ALU.max).then_inc(row_max_done, 1)
                dve.wait_ge(row_max_done, t + 1)
                nc.vector.scalar_tensor_tensor(out=top[:, :], in0=row_max[:, :], scalar=2.0,
                                               in1=c_row[:, bass.ds(t, 1)], op0=ALU.mult,
                                               op1=ALU.add).then_inc(top_done, 1)
                dve.wait_ge(top_done, t + 1)
                nc.vector.scalar_tensor_tensor(out=exp_bias[:, :], in0=c_row[:, bass.ds(t, 1)], scalar=P_SHIFT,
                                               in1=top[:, :], op0=ALU.add, op1=ALU.subtract).then_inc(bias_done, 1)

            def row_sum(t):
                dve.wait_ge(exp_done, t + 1)
                nc.vector.reciprocal(den_r[:, bass.ds(t, 1)], den[:, :]).then_inc(den_r_done, 1)

            def attend(t, b):
                dve.wait_ge(den_r_done, t + 1)
                if not isinstance(t, int) or t > 0:
                    dve.wait_ge(out_ready, t)
                else:
                    dve.wait_ge(x1_done, NT)
                residual(t + NT, xs[:, bass.ds(t, 1), :], b, den_r[:, bass.ds(t, 1)])

            def out_tile(t, b, reuse=True):
                if reuse:
                    dve.wait_ge(out_stored[b], dma_count(t - 2, b))
                normalise(t + NT, out_t[b][:, :], out_ready)

            def y_lo_tile(t, b):
                dve.wait_ge(y_hi_done, t + 1)
                nc.vector.tensor_tensor(yt_lo[b][:, :, :], y_t[:, :, bass.ts(t, P)], yt_hi[b][:, :, :],
                                        ALU.subtract).then_inc(y_lo_done, 1)

            def layer2_step(t, b, z=True, pv=True, y=True, reuse=True):
                if z:
                    attend(t - 2, b)
                if y:
                    y_lo_tile(t + 1, 1 - b)
                for c in range(NG):
                    score_chunk(t, b, c)
                    if c == 0 and pv:
                        row_sum(t - 1)
                    if pv:
                        lo_group((t + (NT - 1)) * NG + c, 1 - b, c, ps_t[c % 2])
                    if z and c == 1:
                        out_tile(t - 2, b, reuse)
                softmax_bias(t)

            y_lo_tile(0, 0)
            y_lo_tile(1, 1)
            xt_lo_tile(NT - 2)
            edge(NT - 1, 1)
            x1_tile(NT - 1, 1)
            v_lo_tile(NT - 2)
            score_chunk(0, 0, 0)
            xt_lo_tile(NT - 1)
            for c in range(1, NG):
                score_chunk(0, 0, c)
            softmax_bias(0)
            v_lo_tile(NT - 1)
            dve.wait_ge(x1_kept, NT)
            layer2_step(1, 1, z=False)
            layer2_step(2, 0, reuse=False)
            layer2_step(3, 1, reuse=False)
            with dve.Fori(4, NT - 3, 2) as t:
                for b in range(2):
                    layer2_step(t + b, b)
            layer2_step(NT - 2, 0)
            layer2_step(NT - 1, 1, y=False)
            row_sum(NT - 1)
            for g in range(NG):
                lo_group((2 * NT - 1) * NG + g, 1, g, ps_s[g])
                if g == 1:
                    attend(NT - 2, 0)
            out_tile(NT - 2, 0)
            attend(NT - 1, 1)
            out_tile(NT - 1, 1)


def kernel(x, adj, L1_gnn_Wq, L1_gnn_bq, L1_gnn_Wk, L1_gnn_bk, L1_gnn_Wv, L1_gnn_bv):
    import concourse.bacc as bacc
    from concourse.bass_utils import run_bass_kernel_spmd

    def blocks(b):
        return np.ascontiguousarray(np.asarray(b).reshape(-1, P).T)

    nc = bacc.Bacc("TRN2", target_bir_lowering=False, num_devices=1)
    arrays = {
        "x": np.ascontiguousarray(x),
        "adj": np.ascontiguousarray(adj),
        "wq": np.ascontiguousarray(L1_gnn_Wq),
        "wk": np.ascontiguousarray(L1_gnn_Wk),
        "wv_t": np.ascontiguousarray(np.asarray(L1_gnn_Wv).T),
        "bq": blocks(L1_gnn_bq),
        "bk": blocks(L1_gnn_bk),
        "bv": np.ascontiguousarray(np.broadcast_to(np.asarray(L1_gnn_bv), (P, L1_gnn_bv.shape[0]))),
    }
    args = [nc.dram_tensor(f"in_{k}", a.shape, mybir.dt.from_np(a.dtype), kind="ExternalInput").ap()
            for k, a in arrays.items()]
    out = nc.dram_tensor("out", arrays["x"].shape, F32, kind="ExternalOutput").ap()
    gnn_layers(nc, *args, out)
    result = run_bass_kernel_spmd(nc, [{f"in_{k}": a for k, a in arrays.items()}], core_ids=[0])
    return result.results[0]["out"]
```
